# Optimizing a Trainium2 kernel written in Bass

```python
import numpy as np
import jax
import jax.numpy as jnp

def _softmax(x, axis=-1):
    return jax.nn.softmax(x, axis=axis)
def _gelu(x):
    return jax.nn.gelu(x, approximate=True)
def _silu(x):
    return jax.nn.silu(x)
def _sigmoid(x):
    return jax.nn.sigmoid(x)
def _layernorm(x, axis=-1, eps=1e-5):
    m = jnp.mean(x, axis=axis, keepdims=True)
    v = jnp.var(x, axis=axis, keepdims=True)
    return (x - m) / jnp.sqrt(v + eps)
def _scatter_add(tgt, idx, src, axis=0):
    return tgt.at[idx].add(src)
def _segment_sum(src, seg, n):
    return jax.ops.segment_sum(src, seg, n)

kernel_name = 'mk_conv_seq_d1_conv_nchw512_6441b8'

def setup_inputs(seed: int = 0):
    np.random.seed(seed)
    _w = jnp.asarray
    def _rec_inputs():
        import jax
        import jax.numpy as jnp
        _gk = jax.random.key(seed)
        x = -7.109e-05 + 0.9999 * jax.random.normal(jax.random.fold_in(_gk, 1), (8, 512, 128, 128), jnp.float32)
        return x
    x = _rec_inputs()
    def _L0_conv_setup():
        import jax, jax.numpy as jnp
        import numpy as np
        IN_DIM = 512
        C_OUT = IN_DIM // 8
        B, H, W = (8, 128, 128)
        key = jax.random.key(seed)
        ks = jax.random.split(key, 6)
        x = jax.random.normal(ks[0], (B, IN_DIM, H, W), dtype=jnp.float32)
        qkv_w = jax.random.normal(ks[1], (3 * C_OUT, IN_DIM), dtype=jnp.float32) * (1.0 / np.sqrt(IN_DIM))
        qkv_b = jax.random.normal(ks[2], (3 * C_OUT,), dtype=jnp.float32) * 0.01
        out_w = jax.random.normal(ks[3], (IN_DIM, C_OUT), dtype=jnp.float32) * (1.0 / np.sqrt(C_OUT))
        out_b = jax.random.normal(ks[4], (IN_DIM,), dtype=jnp.float32) * 0.01
        gamma = jnp.asarray(0.5, dtype=jnp.float32)
        return {'x': x, 'qkv_w': qkv_w, 'qkv_b': qkv_b, 'out_w': out_w, 'out_b': out_b, 'gamma': gamma}
    _L0_conv_all = _L0_conv_setup()
    _L0_conv_in = {k: v for k, v in _L0_conv_all.items() if k in ('qkv_w', 'qkv_b', 'out_w', 'out_b', 'gamma', )}
    del _L0_conv_all

    return {
        "x": x,
        "L0_conv_qkv_w": _L0_conv_in["qkv_w"],
        "L0_conv_qkv_b": _L0_conv_in["qkv_b"],
        "L0_conv_out_w": _L0_conv_in["out_w"],
        "L0_conv_out_b": _L0_conv_in["out_b"],
        "L0_conv_gamma": _L0_conv_in["gamma"],
    }

def reference(x, L0_conv_qkv_w, L0_conv_qkv_b, L0_conv_out_w, L0_conv_out_b, L0_conv_gamma):
    import jax
    import jax.numpy as jnp
    def _L0_conv_ref(x, qkv_w, qkv_b, out_w, out_b, gamma):
        import jax, jax.numpy as jnp
        import numpy as np
        IN_DIM = 512
        C_OUT = IN_DIM // 8
        B, H, W = (8, 128, 128)
        qkv = jnp.einsum('bchw,oc->bohw', x, qkv_w) + qkv_b[None, :, None, None]
        q, k, v = jnp.split(qkv, 3, axis=1)
        energy_h = jnp.einsum('bqhw,bkhw->bwqk', q, k)
        attn_h = jax.nn.softmax(energy_h, axis=-1)
        out_h = jnp.einsum('bwqk,bkhw->bqhw', attn_h, v)
        energy_v = jnp.einsum('bqhw,bkhw->bhqk', q, k)
        attn_v = jax.nn.softmax(energy_v, axis=-1)
        out_v = jnp.einsum('bhqk,bkhw->bqhw', attn_v, v)
        out = gamma * (out_h + out_v)
        out = jnp.einsum('bchw,oc->bohw', out, out_w) + out_b[None, :, None, None]
        return out + x

    def _gn(v, G=32, eps=1e-5):
        B_, C_, H_, W_ = v.shape
        g = v.reshape(B_, G, C_ // G, H_, W_)
        m = jnp.mean(g, axis=(2, 3, 4), keepdims=True)
        s = jnp.var(g, axis=(2, 3, 4), keepdims=True)
        return ((g - m) / jnp.sqrt(s + eps)).reshape(v.shape)

    def _ln_c(v, eps=1e-6):
        m = jnp.mean(v, axis=1, keepdims=True)
        s = jnp.var(v, axis=1, keepdims=True)
        return (v - m) / jnp.sqrt(s + eps)

    def _ln_t(v, eps=1e-5):
        m = jnp.mean(v, axis=-1, keepdims=True)
        s = jnp.var(v, axis=-1, keepdims=True)
        return (v - m) / jnp.sqrt(s + eps)

    def _to_tokens(v):
        B_, C_, H_, W_ = v.shape
        return v.reshape(B_, C_, H_ * W_).transpose(0, 2, 1)
    def _from_tokens(t, like):
        B_, C_, H_, W_ = like.shape
        return t.transpose(0, 2, 1).reshape(B_, C_, H_, W_)

    x = _L0_conv_ref(x, L0_conv_qkv_w, L0_conv_qkv_b, L0_conv_out_w, L0_conv_out_b, L0_conv_gamma)
    return x


_drawn_inputs = setup_inputs


def setup_inputs(seed=0):
    import zlib

    import numpy as np

    out = dict(_drawn_inputs(seed))
    spreads = {}
    factors = {'L0_conv_out_b': 6.883}
    for name, (base, spread) in spreads.items():
        noise = np.random.default_rng([zlib.crc32(name.encode()), seed]).standard_normal(out[name].shape)
        drawn = base * np.exp(spread * noise) if base else spread * noise
        out[name] = jnp.asarray(drawn.astype(out[name].dtype))
    for name, factor in factors.items():
        out[name] = (out[name] * factor).astype(out[name].dtype)
    return out
```

```python
from contextlib import ExitStack

import concourse.bass as bass
from concourse import mybir
from concourse.alu_op_type import AluOpType as ALU

F32 = mybir.dt.float32
F32R = mybir.dt.float32r
ACT = mybir.ActivationFunctionType
AX = mybir.AxisListType

B, C, H, W = 8, 512, 128, 128
D = C // 8
P = 128
KT = C // P
OC = C // P
ROWS = 8
STEPS = H // ROWS
PAIRS = ROWS // 2
HALF = STEPS // 2
CHUNK = 4
SLOTS = 2 * ROWS // CHUNK
CG = 4
NCG = 2 * D // CG
GW = 8
GROUPS = W // GW
GPAIRS = GW // 2
N_WEIGHTS = 8


def axial_attention(nc, x, wqkv_t, qkv_b, wo_t, out_b, gamma, out):
    xk = x.rearrange("b (t p) h w -> b p t (h w)", p=P)
    xo = x.rearrange("b (t p) h w -> b t p (h w)", p=P)
    yo = out.rearrange("b (t p) h w -> b t p (h w)", p=P)

    with ExitStack() as ctx:
        def sb(name, shape, dtype=F32):
            return ctx.enter_context(nc.sbuf_tensor(name, shape, dtype))

        def sem(name):
            return ctx.enter_context(nc.semaphore(name))

        wqkv = sb("wqkv", [P, KT, 3 * D])
        bias_qkv = sb("bias_qkv", [P, 2 * D])
        bias_v = sb("bias_v", [P, 1])
        wo_hi = sb("wo_hi", [P, C], F32R)
        wo_lo = sb("wo_lo", [P, C], F32R)
        bias_o = sb("bias_o", [P, OC])
        gam = sb("gam", [P, 1])
        ident = sb("ident", [P, P])
        QK = sb("QK", [P, H, 2 * D])
        V = sb("V", [P, H // 2, W])
        S = sb("S", [P, H // 2, W])
        x1 = [sb(f"x1_{i}", [P, KT, CHUNK * W]) for i in range(SLOTS)]
        x2 = [sb(f"x2_{o}", [P, ROWS * W]) for o in range(OC)]
        qk_t = sb("qk_t", [P, ROWS, 2 * D])
        s_hl = [sb(f"s_hl{a}", [P, PAIRS * W], F32R) for a in range(2)]
        v_t = sb("v_t", [P, PAIRS, 2, D])
        es = [sb(f"es{i}", [P, GPAIRS, D]) for i in range(2)]
        pr = [sb(f"pr{i}", [P, GPAIRS, D]) for i in range(2)]
        mx = [sb(f"mx{i}", [P, GPAIRS]) for i in range(2)]
        sm = [sb(f"sm{i}", [P, GPAIRS]) for i in range(2)]
        rs = [sb(f"rs{i}", [P, GPAIRS]) for i in range(2)]
        bd = [sb(f"bd{i}", [P, GW, 2 * D]) for i in range(2)]

        wo_raw = qk_t[:, 0:C // (2 * D), :].rearrange("p r d -> p (r d)")

        bank = [ctx.enter_context(nc.psum_tensor(f"bank{i}", [P, 512], F32)) for i in range(2)]
        proj_ps = ctx.enter_context(nc.psum_tensor("proj_ps", [P, 2, 512], F32))
        bank += [proj_ps[:, 0, :], proj_ps[:, 1, :]]
        bank += [ctx.enter_context(nc.psum_tensor(f"bank{i}", [P, 512], F32)) for i in range(4, 8)]
        vt_ps, e_ps, pt_ps, ov_ps = bank[4:8]
        e_bank, pt_bank, oh_bank = (bank[5], bank[4]), (bank[6], bank[0]), (bank[7], bank[1])

        weights_loaded = sem("weights_loaded")
        ident_zero = sem("ident_zero")
        ident_ready = sem("ident_ready")
        consts_ready = sem("consts_ready")
        x1_loaded = [sem(f"x1_loaded{i}") for i in range(SLOTS)]
        x2_loaded = [sem(f"x2_loaded{o}") for o in range(OC)]
        stored = [sem(f"stored{o}") for o in range(OC)]
        qkv_done = sem("qkv_done")
        qk_kept = sem("qk_kept")
        qk_stored = sem("qk_stored")
        v_kept = sem("v_kept")
        vt_done = sem("vt_done")
        v_stored = sem("v_stored")
        ev_done = sem("ev_done")
        v_max = sem("v_max")
        v_sub = sem("v_sub")
        v_exp = sem("v_exp")
        v_sum = sem("v_sum")
        v_rs = sem("v_rs")
        pv_done = sem("pv_done")
        bdv_ready = sem("bdv_ready")
        ov_done = sem("ov_done")
        s_set = sem("s_set")
        s_hi = sem("s_hi")
        s_lo = sem("s_lo")
        proj_done = sem("proj_done")
        added = sem("added")
        ch_done = sem("ch_done")
        ch_kept_dve = sem("ch_kept_dve")
        ch_kept_act = sem("ch_kept_act")
        eh_done = sem("eh_done")
        h_max = sem("h_max")
        h_sub = sem("h_sub")
        h_exp = sem("h_exp")
        h_sum = sem("h_sum")
        h_rs = sem("h_rs")
        h_norm = sem("h_norm")
        ph_done = sem("ph_done")
        bdh_ready = [sem(f"bdh_ready{i}") for i in range(2)]
        oh_done = sem("oh_done")
        s_added = sem("s_added")

        block = ctx.enter_context(nc.Block())

        @block.sync
        def _(sp):
            sp.dma_start(wqkv[:], wqkv_t.rearrange("(t p) o -> p t o", p=P)).then_inc(weights_loaded, 16)
            sp.dma_start(bias_qkv[:], qkv_b[0:2 * D].partition_broadcast(P)).then_inc(weights_loaded, 16)
            bv = qkv_b[2 * D:3 * D].rearrange("(d o) -> d o", o=1)
            sp.dma_start(bias_v[0:D, :], bv).then_inc(weights_loaded, 16)
            sp.dma_start(bias_v[D:P, :], bv).then_inc(weights_loaded, 16)
            for a in range(2):
                sp.dma_start(wo_raw[a * D:(a + 1) * D, :], wo_t).then_inc(weights_loaded, 16)
            sp.dma_start(bias_o[:], out_b).then_inc(weights_loaded, 16)
            sp.dma_start(gam[:], gamma.partition_broadcast(P)).then_inc(weights_loaded, 16)

            def step(b, s):
                t = b * STEPS + s
                for o in range(OC):
                    sp.wait_ge(stored[o], 16 * t)
                    sp.dma_start(x2[o][:], xo[b, o, :, bass.ds(s * (ROWS * W), ROWS * W)]).then_inc(x2_loaded[o], 16)
                for o in range(OC):
                    sp.wait_ge(added, OC * t + o + 1)
                    sp.dma_start(yo[b, o, :, bass.ds(s * (ROWS * W), ROWS * W)], x2[o][:]).then_inc(stored[o], 16)

            with sp.Fori(0, B) as b, sp.Fori(0, STEPS) as s:
                step(b, s)
            for o in range(OC):
                sp.wait_ge(stored[o], 16 * B * STEPS)

        @block.gpsimd
        def _(pool):
            nc.gpsimd.memset(ident[:], 0.0).then_inc(ident_zero, 1)
            pool.wait_ge(ident_zero, 1)
            nc.gpsimd.affine_select(out=ident[:], in_=ident[:], compare_op=ALU.not_equal, fill=1.0, base=0,
                                    pattern=[[-1, P]], channel_multiplier=1).then_inc(ident_ready, 1)
            with pool.Fori(0, B) as b:
                with pool.Fori(0, STEPS) as s:
                    pool.wait_ge(qk_kept, (b * STEPS + s + 1) * PAIRS)
                    nc.gpsimd.tensor_copy(QK[:, bass.ds(s * ROWS, ROWS), :], qk_t[:]).then_inc(qk_stored, 1)
                with pool.Fori(0, GROUPS // 2) as i:
                    for k in range(2):
                        pool.wait_ge(h_rs, b * GROUPS + i * 2 + k + 1)
                        nc.gpsimd.tensor_tensor(pr[k][:], pr[k][:],
                                                rs[k][:].unsqueeze(2).broadcast_to([P, GPAIRS, D]),
                                                ALU.mult).then_inc(h_norm, 1)

        @block.tensor
        def _(pe):
            bdv_due = pe.alloc_register("bdv_due")
            bdh_due = [pe.alloc_register(f"bdh_due{i}") for i in range(2)]
            pe.reg_mov(bdv_due, 0)
            for due in bdh_due:
                pe.reg_mov(due, 0)

            def project(b, s, o):
                t = b * STEPS + s
                if o == 0:
                    pe.wait_ge(s_lo, 2 * t + 2)
                pe.wait_ge(added, OC * t + o)
                for a in range(2):
                    for k, w in enumerate((wo_hi, wo_lo)):
                        last = nc.tensor.matmul(proj_ps[:, a, :], w[:, o * P:(o + 1) * P], s_hl[a][:],
                                                start=(k == 0), stop=(k == 1))
                last.then_inc(proj_done, 1)

            def step(b, s2, u, second):
                s = s2 * 2 + u
                t = b * STEPS + s
                for p in range(PAIRS):
                    slot = 2 * u + p // 2
                    if p % 2 == 0:
                        pe.wait_ge(x1_loaded[slot], (b * HALF + s2 + 1) * 16)
                    pe.wait_ge(v_kept, t * PAIRS + max(p - 1, 0))
                    for r in range(2):
                        at = (2 * (p % 2) + r) * W
                        for k in range(KT):
                            last = nc.tensor.matmul(bank[p % 2][:, r * 3 * D:(r + 1) * 3 * D],
                                                    x1[slot][:, k, at:at + W], wqkv[:, k, :],
                                                    start=(k == 0), stop=(k == KT - 1))
                    last.then_inc(qkv_done, 1)
                if second:
                    project(b - 1, s, 0)
                pe.wait_ge(v_kept, (t + 1) * PAIRS)
                pe.wait_ge(v_stored, t)
                for j in range(PAIRS):
                    last = nc.tensor.transpose(vt_ps[:, j * P:(j + 1) * P], v_t[:, j, :, :], ident[:])
                last.then_inc(vt_done, 1)
                pe.wait_ge(qk_kept, (t + 1) * PAIRS)
                pe.wait_ge(v_sub, t)
                for j in range(PAIRS):
                    for a in range(2):
                        row = a * PAIRS + j
                        last = nc.tensor.matmul(e_ps[a * D:(a + 1) * D, j * D:(j + 1) * D],
                                                qk_t[:, row, 0:D], qk_t[:, row, D:2 * D],
                                                start=True, stop=True)
                last.then_inc(ev_done, 1)
                if second:
                    project(b - 1, s, 1)
                    project(b - 1, s, 2)
                pe.wait_ge(v_exp, t + 1)
                pe.reg_add(bdv_due, bdv_due, 2)
                for j in range(PAIRS):
                    last = nc.tensor.transpose(pt_ps[0:D, j * P:(j + 1) * P], pr[0][:, j, :], ident[:])
                last.then_inc(pv_done, 1)
                if second:
                    project(b - 1, s, 3)
                pe.wait_ge(bdv_ready, bdv_due)
                pe.wait_ge(v_stored, t + 1)
                pe.wait_ge(s_set, t)
                for j in range(PAIRS):
                    last = nc.tensor.matmul(ov_ps[:, j * W:(j + 1) * W], bd[0][:, j, :],
                                            V[:, bass.ds(s * PAIRS + j, 1), :], start=True, stop=True)
                last.then_inc(ov_done, 1)

            def energies(b, i, k):
                g = i * 2 + k
                n = b * GROUPS + g
                if k:
                    pe.wait_ge(h_sub, n - 1)
                else:
                    pe.wait_ge(h_sub, n)
                for j in range(GPAIRS):
                    for a in range(2):
                        col = g * GW + 2 * j + a
                        last = nc.tensor.matmul(e_bank[k][a * D:(a + 1) * D, j * D:(j + 1) * D],
                                                QK[:, col, 0:D], QK[:, col, D:2 * D],
                                                start=True, stop=True)
                last.then_inc(eh_done, 1)

            def probs_t(b, i, k):
                n = b * GROUPS + i * 2 + k
                pe.wait_ge(h_norm, n + 1)
                pe.reg_add(bdh_due[k], bdh_due[k], 2)
                for j in range(GPAIRS):
                    last = nc.tensor.transpose(pt_bank[k][0:D, j * P:(j + 1) * P], pr[k][:, j, :], ident[:])
                last.then_inc(ph_done, 1)

            def apply(b, i, k):
                g = i * 2 + k
                n = b * GROUPS + g
                pe.wait_ge(bdh_ready[k], bdh_due[k])
                if k:
                    pe.wait_ge(s_added, n - 1)
                else:
                    pe.wait_ge(s_added, n)
                for w in range(GW):
                    last = nc.tensor.matmul(oh_bank[k][:, w * D:(w + 1) * D], bd[k][:, w, :],
                                            V[:, :, g * GW + w], start=True, stop=True)
                last.then_inc(oh_done, 1)

            def middle(b):
                pe.wait_ge(v_kept, (b + 1) * STEPS * PAIRS)
                pe.wait_ge(added, b * STEPS * OC)
                pe.wait_ge(qk_stored, (b + 1) * STEPS)
                for i in range(NCG // 4):
                    for q in range(4):
                        pe.wait_ge((ch_kept_dve, ch_kept_act)[q % 2], b * (NCG // 2) + i * 2)
                        for c in range(CG):
                            ch = (i * 4 + q) * CG + c
                            last = nc.tensor.transpose(bank[q][:, c * P:(c + 1) * P], QK[:, :, ch], ident[:])
                        last.then_inc(ch_done, 1)
                pe.wait_ge(ch_kept_dve, (b + 1) * (NCG // 2))
                pe.wait_ge(ch_kept_act, (b + 1) * (NCG // 2))
                pe.wait_ge(s_set, (b + 1) * STEPS)
                pe.wait_ge(v_stored, (b + 1) * STEPS)
                for k in range(2):
                    energies(b, 0, k)
                last_i = GROUPS // 2 - 1
                for i in range(last_i):
                    probs_t(b, i, 0)
                    energies(b, i + 1, 0)
                    probs_t(b, i, 1)
                    apply(b, i, 0)
                    energies(b, i + 1, 1)
                    apply(b, i, 1)
                probs_t(b, last_i, 0)
                probs_t(b, last_i, 1)
                apply(b, last_i, 0)
                apply(b, last_i, 1)
                pe.wait_ge(s_added, (b + 1) * GROUPS)

            pe.wait_ge(weights_loaded, 16 * N_WEIGHTS)
            pe.wait_ge(ident_ready, 1)
            pe.wait_ge(consts_ready, 5)
            with pe.Fori(0, HALF) as s2:
                for u in range(2):
                    step(0, s2, u, False)
            middle(0)
            with pe.Fori(1, B) as b:
                with pe.Fori(0, HALF) as s2:
                    for u in range(2):
                        step(b, s2, u, True)
                middle(b)
            with pe.Fori(0, STEPS) as s:
                for o in range(OC):
                    project(B - 1, s, o)

        @block.scalar
        def _(act):
            def load_x1(b, s, u):
                for h in range(2):
                    act.dma_start(x1[2 * u + h][:], xk[b, :, :, bass.ds(s * (ROWS * W) + h * CHUNK * W, CHUNK * W)])\
                       .then_inc(x1_loaded[2 * u + h], 16)

            def high_parts(b, s):
                t = b * STEPS + s
                act.wait_ge(s_added, (b + 1) * GROUPS)
                act.wait_ge(proj_done, OC * t)
                for a in range(2):
                    half = slice(a * D, (a + 1) * D)
                    nc.scalar.activation(s_hl[a][half, :], S[half, bass.ds(s * PAIRS, PAIRS), :]
                                         .rearrange("p j w -> p (j w)"), ACT.Copy).then_inc(s_hi, 1)

            def step(b, s2, u, ahead, second):
                s = s2 * 2 + u
                t = b * STEPS + s
                if second:
                    high_parts(b - 1, s)
                act.wait_ge(vt_done, t)
                for p in range(PAIRS):
                    act.wait_ge(qk_kept, t * PAIRS + p + 1)
                    nc.scalar.activation(v_t[:, 2 * (p % 2):2 * (p % 2) + 2, p // 2, :],
                                         bank[p % 2][:, 0:6 * D].rearrange("p (r d) -> p r d", r=2)[:, :, 2 * D:],
                                         ACT.Copy).then_inc(v_kept, 1)
                if ahead:
                    load_x1(b, s + 2, u)
                act.wait_ge(vt_done, t + 1)
                nc.scalar.activation(V[:, bass.ds(s * PAIRS, PAIRS), :],
                                     vt_ps[:].rearrange("p (j w) -> p j w", j=PAIRS),
                                     ACT.Identity, bias=bias_v[:]).then_inc(v_stored, 1)
                act.wait_ge(v_sub, t + 1)
                act.wait_ge(pv_done, t)
                nc.scalar.activation(pr[0][:], es[0][:], ACT.Exp).then_inc(v_exp, 1)
                act.wait_ge(pv_done, t + 1)
                act.wait_ge(ov_done, t)
                pt = pt_ps[0:D, :].rearrange("p (j a d) -> p j a d", j=PAIRS, a=2)
                for a in range(2):
                    nc.scalar.activation(bd[0][a * D:(a + 1) * D, 0:PAIRS, a * D:(a + 1) * D], pt[:, :, a, :],
                                         ACT.Copy).then_inc(bdv_ready, 1)

            def exps(b, i, k):
                n = b * GROUPS + i * 2 + k
                act.wait_ge(h_sub, n + 1)
                nc.scalar.activation(pr[k][:], es[k][:], ACT.Exp).then_inc(h_exp, 1)

            def diagonal(b, i, k):
                n = b * GROUPS + i * 2 + k
                act.wait_ge(ph_done, n + 1)
                if k:
                    act.wait_ge(oh_done, n - 1)
                else:
                    act.wait_ge(oh_done, n)
                pt = pt_bank[k][0:D, :].rearrange("p (w d) -> p w d", w=GW)
                for a in range(2):
                    nc.scalar.activation(bd[k][a * D:(a + 1) * D, :, a * D:(a + 1) * D], pt, ACT.Copy)\
                      .then_inc(bdh_ready[k], 1)

            def middle(b, ahead):
                if ahead:
                    load_x1(b + 1, 0, 0)
                    load_x1(b + 1, 1, 1)
                with act.Fori(0, NCG // 4) as i:
                    for q in (1, 3):
                        act.wait_ge(ch_done, b * NCG + i * 4 + q + 1)
                        nc.scalar.activation(QK[:, :, bass.ds((i * 4 + q) * CG, CG)],
                                             bank[q][:, :].rearrange("p (c w) -> p w c", c=CG),
                                             ACT.Copy).then_inc(ch_kept_act, 1)
                for k in range(2):
                    exps(b, 0, k)
                last_i = GROUPS // 2 - 1
                with act.Fori(0, last_i) as i:
                    for k in range(2):
                        diagonal(b, i, k)
                        exps(b, i + 1, k)
                for k in range(2):
                    diagonal(b, last_i, k)

            def image(b, ahead, second):
                with act.Fori(0, HALF - 1) as s2:
                    for u in range(2):
                        step(b, s2, u, True, second)
                for u in range(2):
                    step(b, HALF - 1, u, False, second)
                middle(b, ahead)

            for u in range(2):
                load_x1(0, u, u)
            act.wait_ge(weights_loaded, 16 * N_WEIGHTS)
            act.wait_ge(consts_ready, 3)
            image(0, True, False)
            with act.Fori(1, B - 1) as b:
                image(b, True, True)
            image(B - 1, False, True)
            with act.Fori(0, STEPS) as s:
                high_parts(B - 1, s)

        @block.vector
        def _(dve):
            bias2 = bias_qkv[:].unsqueeze(1).broadcast_to([P, 2, 2 * D])

            def over(v, n):
                return v[:].unsqueeze(2).broadcast_to([P, GPAIRS, n])

            def add_x(b, s, o):
                t = b * STEPS + s
                dve.wait_ge(proj_done, OC * t + o + 1)
                dve.wait_ge(x2_loaded[o], (t + 1) * 16)
                nc.vector.scalar_tensor_tensor(out=x2[o][:], in0=proj_ps[:, :, :].rearrange("p a n -> p (a n)"),
                                               scalar=bias_o[:, o:o + 1], in1=x2[o][:],
                                               op0=ALU.add, op1=ALU.add).then_inc(added, 1)

            def low_parts(b, s):
                t = b * STEPS + s
                for a in range(2):
                    dve.wait_ge(s_hi, 2 * t + a + 1)
                    half, other = slice(a * D, (a + 1) * D), slice((1 - a) * D, (2 - a) * D)
                    nc.vector.tensor_tensor(s_hl[a][other, :], S[half, bass.ds(s * PAIRS, PAIRS), :]
                                            .rearrange("p j w -> p (j w)"), s_hl[a][half, :].bitcast(F32),
                                            ALU.subtract).then_inc(s_lo, 1)

            def step(b, s2, u, second):
                s = s2 * 2 + u
                t = b * STEPS + s
                if second:
                    low_parts(b - 1, s)
                dve.wait_ge(ev_done, t)
                dve.wait_ge(qk_stored, t)
                for p in range(PAIRS):
                    dve.wait_ge(qkv_done, t * PAIRS + p + 1)
                    nc.vector.tensor_tensor(qk_t[:, 2 * p:2 * p + 2, :],
                                            bank[p % 2][:, 0:6 * D].rearrange("p (r d) -> p r d", r=2)[:, :, 0:2 * D],
                                            bias2, ALU.add).then_inc(qk_kept, 1)
                if second:
                    add_x(b - 1, s, 0)
                dve.wait_ge(ev_done, t + 1)
                e = e_ps[:, 0:PAIRS * D].rearrange("p (j d) -> p j d", j=PAIRS)
                nc.vector.tensor_reduce(mx[0][:], e, axis=AX.X, op=ALU.max).then_inc(v_max, 1)
                dve.wait_ge(v_max, t + 1)
                dve.wait_ge(v_exp, t)
                nc.vector.tensor_tensor(es[0][:], e, over(mx[0], D), ALU.subtract).then_inc(v_sub, 1)
                if second:
                    add_x(b - 1, s, 1)
                dve.wait_ge(v_exp, t + 1)
                nc.vector.tensor_reduce(sm[0][:], pr[0][:], axis=AX.X, op=ALU.add).then_inc(v_sum, 1)
                dve.wait_ge(v_sum, t + 1)
                nc.vector.reciprocal(rs[0][:], sm[0][:]).then_inc(v_rs, 1)
                if second:
                    add_x(b - 1, s, 2)
                    add_x(b - 1, s, 3)
                dve.wait_ge(v_rs, t + 1)
                dve.wait_ge(ov_done, t + 1)
                nc.vector.tensor_tensor(S[:, bass.ds(s * PAIRS, PAIRS), :],
                                        ov_ps[:].rearrange("p (j w) -> p j w", j=PAIRS),
                                        over(rs[0], W), ALU.mult).then_inc(s_set, 1)

            def shifted(b, i, k):
                n = b * GROUPS + i * 2 + k
                dve.wait_ge(eh_done, n + 1)
                e = e_bank[k][:, 0:GPAIRS * D].rearrange("p (j d) -> p j d", j=GPAIRS)
                nc.vector.tensor_reduce(mx[k][:], e, axis=AX.X, op=ALU.max).then_inc(h_max, 1)
                dve.wait_ge(h_max, n + 1)
                nc.vector.tensor_tensor(es[k][:], e, over(mx[k], D), ALU.subtract).then_inc(h_sub, 1)

            def sums(b, i, k):
                n = b * GROUPS + i * 2 + k
                dve.wait_ge(h_exp, n + 1)
                nc.vector.tensor_reduce(sm[k][:], pr[k][:], axis=AX.X, op=ALU.add).then_inc(h_sum, 1)
                dve.wait_ge(h_sum, n + 1)
                nc.vector.reciprocal(rs[k][:], sm[k][:]).then_inc(h_rs, 1)

            def add_s(b, i, k):
                g = i * 2 + k
                n = b * GROUPS + g
                dve.wait_ge(oh_done, n + 1)
                cols = S[:, :, bass.ds(g * GW, GW)]
                nc.vector.tensor_tensor(cols, oh_bank[k][:].rearrange("p (w j) -> p j w", w=GW), cols,
                                        ALU.add).then_inc(s_added, 1)

            def middle(b):
                with dve.Fori(0, NCG // 4) as i:
                    for q in (0, 2):
                        dve.wait_ge(ch_done, b * NCG + i * 4 + q + 1)
                        nc.vector.tensor_copy(QK[:, :, bass.ds((i * 4 + q) * CG, CG)],
                                              bank[q][:, :].rearrange("p (c w) -> p w c", c=CG))\
                          .then_inc(ch_kept_dve, 1)
                dve.wait_ge(s_set, (b + 1) * STEPS)
                for k in range(2):
                    shifted(b, 0, k)
                for k in range(2):
                    sums(b, 0, k)
                last_i = GROUPS // 2 - 1
                with dve.Fori(0, last_i) as i:
                    shifted(b, i + 1, 0)
                    add_s(b, i, 0)
                    sums(b, i + 1, 0)
                    shifted(b, i + 1, 1)
                    add_s(b, i, 1)
                    sums(b, i + 1, 1)
                for k in range(2):
                    add_s(b, last_i, k)

            nc.vector.memset(bd[0][:], 0.0).then_inc(consts_ready, 1)
            nc.vector.memset(bd[1][:], 0.0).then_inc(consts_ready, 1)
            dve.wait_ge(weights_loaded, 16 * N_WEIGHTS)
            nc.vector.tensor_scalar(wo_raw, wo_raw, gam[:], None, ALU.mult).then_inc(consts_ready, 1)
            dve.wait_ge(consts_ready, 3)
            nc.vector.tensor_copy(wo_hi[:], wo_raw).then_inc(consts_ready, 1)
            dve.wait_ge(consts_ready, 4)
            nc.vector.tensor_tensor(wo_lo[:], wo_raw, wo_hi[:].bitcast(F32), ALU.subtract).then_inc(consts_ready, 1)
            dve.wait_ge(consts_ready, 5)
            with dve.Fori(0, HALF) as s2:
                for u in range(2):
                    step(0, s2, u, False)
            middle(0)
            with dve.Fori(1, B) as b:
                with dve.Fori(0, HALF) as s2:
                    for u in range(2):
                        step(b, s2, u, True)
                middle(b)
            with dve.Fori(0, STEPS) as s:
                low_parts(B - 1, s)
                for o in range(OC):
                    add_x(B - 1, s, o)


def kernel(x, L0_conv_qkv_w, L0_conv_qkv_b, L0_conv_out_w, L0_conv_out_b, L0_conv_gamma):
    import numpy as np
    import concourse.bacc as bacc
    from concourse.bass_utils import run_bass_kernel_spmd

    arrays = {
        "x": np.ascontiguousarray(x),
        "wqkv_t": np.ascontiguousarray(np.asarray(L0_conv_qkv_w).T),
        "qkv_b": np.ascontiguousarray(L0_conv_qkv_b),
        "wo_t": np.ascontiguousarray(np.asarray(L0_conv_out_w).T),
        "out_b": np.ascontiguousarray(np.asarray(L0_conv_out_b).reshape(OC, P).T),
        "gamma": np.ascontiguousarray(L0_conv_gamma).reshape(1),
    }
    nc = bacc.Bacc("TRN2", target_bir_lowering=False, num_devices=1)
    aps = [nc.dram_tensor(n, a.shape, mybir.dt.from_np(a.dtype), kind="ExternalInput").ap() for n, a in arrays.items()]
    out = nc.dram_tensor("out", (B, C, H, W), F32, kind="ExternalOutput").ap()
    axial_attention(nc, *aps, out)
    r = run_bass_kernel_spmd(nc, [arrays], core_ids=[0])
    return r.results[0]["out"]
```

```python
from contextlib import ExitStack

import concourse.bass as bass
from concourse import mybir
from concourse.alu_op_type import AluOpType as ALU

F32 = mybir.dt.float32
F32R = mybir.dt.float32r
ACT = mybir.ActivationFunctionType
AX = mybir.AxisListType

B, C, H, W = 8, 512, 128, 128
D = C // 8
P = 128
KT = C // P
OC = C // P
ROWS = 8
STEPS = H // ROWS
PAIRS = ROWS // 2
CHUNK = 4
SLOTS = ROWS // CHUNK
LATE = 4
EARLY = STEPS - LATE
CG = 4
NCG = 2 * D // CG
GW = 8
GROUPS = W // GW
TURNS = GROUPS // 2
GPAIRS = GW // 2
SETS = 4
N_WEIGHTS = 8


def axial_attention(nc, x, wqkv_t, qkv_b, wo_t, out_b, gamma, out):
    xk = x.rearrange("b (t p) h w -> b p t (h w)", p=P)
    xo = x.rearrange("b (t p) h w -> b t p (h w)", p=P)
    yo = out.rearrange("b (t p) h w -> b t p (h w)", p=P)

    with ExitStack() as ctx:
        def sb(name, shape, dtype=F32):
            return ctx.enter_context(nc.sbuf_tensor(name, shape, dtype))

        def sem(name):
            return ctx.enter_context(nc.semaphore(name))

        wqkv = sb("wqkv", [P, KT, 3 * D])
        bias_qkv = sb("bias_qkv", [P, 2 * D])
        bias_v = sb("bias_v", [P, 1])
        wo_hi = sb("wo_hi", [P, C], F32R)
        wo_lo = sb("wo_lo", [P, C], F32R)
        bias_o = sb("bias_o", [P, OC])
        gam = sb("gam", [P, 1])
        ident = sb("ident", [P, P])
        QK = sb("QK", [P, H, 2 * D])
        V = sb("V", [P, H // 2, W])
        S = sb("S", [P, H // 2, W])
        S_late = sb("S_late", [P, LATE * PAIRS, W])
        x1 = [sb(f"x1_{i}", [P, KT, CHUNK * W]) for i in range(SLOTS)]
        x2 = [sb(f"x2_{o}", [P, ROWS * W]) for o in range(OC)]
        x_end = [[QK[:, (n * OC + o) * ROWS:(n * OC + o + 1) * ROWS, :].rearrange("p r d -> p (r d)")
                  for o in range(OC)] for n in range(SETS)]
        qk_t = sb("qk_t", [P, ROWS, 2 * D])
        s_hl = [sb(f"s_hl{a}", [P, PAIRS * W], F32R) for a in range(2)]
        v_t = sb("v_t", [P, PAIRS, 2, D])
        es = [sb(f"es{i}", [P, GPAIRS, D]) for i in range(2)]
        pr = [sb(f"pr{i}", [P, GPAIRS, D]) for i in range(2)]
        mx = [sb(f"mx{i}", [P, GPAIRS]) for i in range(2)]
        sm = [sb(f"sm{i}", [P, GPAIRS]) for i in range(2)]
        rs = [sb(f"rs{i}", [P, GPAIRS]) for i in range(2)]
        bd = sb("bd", [P, PAIRS, 2 * D])
        pt = [sb(f"pt{i}", [P, GW, D]) for i in range(2)]
        wo_raw = qk_t[:, 0:C // (2 * D), :].rearrange("p r d -> p (r d)")

        bank = [ctx.enter_context(nc.psum_tensor(f"bank{i}", [P, 512], F32)) for i in range(2)]
        proj_ps = ctx.enter_context(nc.psum_tensor("proj_ps", [P, 2, 512], F32))
        bank += [proj_ps[:, 0, :], proj_ps[:, 1, :]]
        bank += [ctx.enter_context(nc.psum_tensor(f"bank{i}", [P, 512], F32)) for i in range(4, 8)]
        vt_ps, e_ps, pt_ps, ov_ps = bank[4:8]
        ch_bank = (bank[0], bank[1], bank[4], bank[5])
        e_bank, pt_bank, oh_bank = (bank[5], bank[4]), (bank[6], bank[0]), (bank[7], bank[1])

        weights_loaded = sem("weights_loaded")
        ident_zero = sem("ident_zero")
        ident_ready = sem("ident_ready")
        consts_ready = sem("consts_ready")
        x1_loaded = [sem(f"x1_loaded{i}") for i in range(SLOTS)]
        x2_loaded = [sem(f"x2_loaded{o}") for o in range(OC)]
        stored = [sem(f"stored{o}") for o in range(OC)]
        end_loaded = [[sem(f"end_loaded{n}_{o}") for o in range(OC)] for n in range(SETS)]
        end_stored = [[sem(f"end_stored{n}_{o}") for o in range(OC)] for n in range(SETS)]
        qkv_done = sem("qkv_done")
        qk_kept = sem("qk_kept")
        qk_stored = sem("qk_stored")
        v_kept = sem("v_kept")
        vt_done = sem("vt_done")
        v_stored = sem("v_stored")
        ev_done = sem("ev_done")
        v_max = sem("v_max")
        v_sub = sem("v_sub")
        v_exp = sem("v_exp")
        v_sum = sem("v_sum")
        v_rs = sem("v_rs")
        pv_done = sem("pv_done")
        bd_ready = sem("bd_ready")
        ov_done = sem("ov_done")
        s_set = sem("s_set")
        late_kept = sem("late_kept")
        s_hi = sem("s_hi")
        s_lo = sem("s_lo")
        proj_done = sem("proj_done")
        added = sem("added")
        ch_done = sem("ch_done")
        ch_kept_dve = sem("ch_kept_dve")
        ch_kept_act = sem("ch_kept_act")
        eh_done = sem("eh_done")
        h_max = sem("h_max")
        h_sub = [sem(f"h_sub{i}") for i in range(2)]
        h_exp = sem("h_exp")
        h_sum = sem("h_sum")
        h_rs = sem("h_rs")
        h_norm = sem("h_norm")
        ph_done = sem("ph_done")
        pt_ready = [sem(f"pt_ready{i}") for i in range(2)]
        oh_done = [sem(f"oh_done{i}") for i in range(2)]
        s_added = [sem(f"s_added{i}") for i in range(2)]

        def opened(engine, *sems):
            for one in sems:
                engine.sem_inc(one, 1)

        def late_units(i):
            return [(1 + i // 2, 2 * (i % 2) + o) for o in range(2)] if i // 2 + 1 < LATE else []

        block = ctx.enter_context(nc.Block())

        @block.sync
        def _(sp):
            sp.dma_start(wqkv[:], wqkv_t.rearrange("(t p) o -> p t o", p=P)).then_inc(weights_loaded, 16)
            sp.dma_start(bias_qkv[:], qkv_b[0:2 * D].partition_broadcast(P)).then_inc(weights_loaded, 16)
            bv = qkv_b[2 * D:3 * D].rearrange("(d o) -> d o", o=1)
            for a in range(2):
                sp.dma_start(bias_v[a * D:(a + 1) * D, :], bv).then_inc(weights_loaded, 16)
                sp.dma_start(wo_raw[a * D:(a + 1) * D, :], wo_t).then_inc(weights_loaded, 16)
            sp.dma_start(bias_o[:], out_b).then_inc(weights_loaded, 16)
            sp.dma_start(gam[:], gamma.partition_broadcast(P)).then_inc(weights_loaded, 16)
            opened(sp, *stored)

            with sp.Fori(0, B - 1) as b, sp.Fori(0, STEPS) as s:
                t = b * STEPS + s
                for o in range(OC):
                    sp.wait_ge(stored[o], 16 * t + 1)
                    sp.dma_start(x2[o][:], xo[b, o, :, bass.ds(s * (ROWS * W), ROWS * W)]).then_inc(x2_loaded[o], 16)
                for o in range(OC):
                    sp.wait_ge(added, OC * t + o + 2)
                    sp.dma_start(yo[b, o, :, bass.ds(s * (ROWS * W), ROWS * W)], x2[o][:]).then_inc(stored[o], 16)

            sp.wait_ge(eh_done, B * GROUPS + 1)
            for n in range(SETS):
                for o in range(OC):
                    sp.dma_start(x_end[n][o], xo[B - 1, o, :, n * ROWS * W:(n + 1) * ROWS * W])\
                      .then_inc(end_loaded[n][o], 16)
            with sp.Fori(0, STEPS // SETS - 1) as r:
                for n in range(SETS):
                    t = (B - 1) * STEPS + r * SETS + n
                    at = (r * SETS + n) * (ROWS * W)
                    for o in range(OC):
                        sp.wait_ge(added, OC * t + o + 2)
                        sp.dma_start(yo[B - 1, o, :, bass.ds(at, ROWS * W)], x_end[n][o]).then_inc(end_stored[n][o], 16)
                    for o in range(OC):
                        sp.wait_ge(end_stored[n][o], 16 * (r + 1))
                        sp.dma_start(x_end[n][o], xo[B - 1, o, :, bass.ds(at + SETS * ROWS * W, ROWS * W)])\
                          .then_inc(end_loaded[n][o], 16)
            for n in range(SETS):
                s = STEPS - SETS + n
                for o in range(OC):
                    sp.wait_ge(added, OC * ((B - 1) * STEPS + s) + o + 2)
                    sp.dma_start(yo[B - 1, o, :, s * ROWS * W:(s + 1) * ROWS * W], x_end[n][o])\
                      .then_inc(end_stored[n][o], 16)
            for o in range(OC):
                sp.wait_ge(stored[o], 16 * (B - 1) * STEPS + 1)
                for n in range(SETS):
                    sp.wait_ge(end_stored[n][o], 16 * (STEPS // SETS))

        @block.gpsimd
        def _(pool):
            nc.gpsimd.memset(ident[:], 0.0).then_inc(ident_zero, 1)
            pool.wait_ge(ident_zero, 1)
            nc.gpsimd.affine_select(out=ident[:], in_=ident[:], compare_op=ALU.not_equal, fill=1.0, base=0,
                                    pattern=[[-1, P]], channel_multiplier=1).then_inc(ident_ready, 1)
            opened(pool, qk_stored, late_kept, h_norm)

            def image(b, second):
                if second:
                    with pool.Fori(0, LATE) as n:
                        for k in range(2):
                            pool.wait_ge(s_added[k], b * TURNS + 1)
                        pool.wait_ge(s_lo, 2 * STEPS * (b - 1) + 1)
                        nc.gpsimd.tensor_copy(S_late[:, bass.ds(n * PAIRS, PAIRS), :],
                                              S[:, bass.ds((n + EARLY) * PAIRS, PAIRS), :]).then_inc(late_kept, 1)
                with pool.Fori(0, STEPS) as s:
                    pool.wait_ge(qk_kept, (b * STEPS + s + 1) * PAIRS + 1)
                    nc.gpsimd.tensor_copy(QK[:, bass.ds(s * ROWS, ROWS), :], qk_t[:]).then_inc(qk_stored, 1)
                with pool.Fori(0, TURNS) as i:
                    for k in range(2):
                        pool.wait_ge(h_rs, b * GROUPS + i * 2 + k + 2)
                        nc.gpsimd.tensor_tensor(pr[k][:], pr[k][:],
                                                rs[k][:].unsqueeze(2).broadcast_to([P, GPAIRS, D]),
                                                ALU.mult).then_inc(h_norm, 1)

            image(0, False)
            with pool.Fori(1, B) as b:
                image(b, True)

        @block.tensor
        def _(pe):
            bd_due = pe.alloc_register("bd_due")
            pt_due = [pe.alloc_register(f"pt_due{k}") for k in range(2)]
            s_due = [pe.alloc_register(f"s_due{k}") for k in range(2)]
            for due in (bd_due, *pt_due, *s_due):
                pe.reg_mov(due, 1)

            def project(b, s, o):
                t = b * STEPS + s
                if o == 0:
                    pe.wait_ge(s_lo, 2 * t + 3)
                pe.wait_ge(added, OC * t + o + 1)
                for a in range(2):
                    for k, w in enumerate((wo_hi, wo_lo)):
                        last = nc.tensor.matmul(proj_ps[:, a, :], w[:, o * P:(o + 1) * P], s_hl[a][:],
                                                start=(k == 0), stop=(k == 1))
                last.then_inc(proj_done, 1)

            def qkv(b, s, p):
                t = b * STEPS + s
                slot = 2 * p // CHUNK
                if 2 * p % CHUNK == 0:
                    pe.wait_ge(x1_loaded[slot], (t + 1) * 16)
                pe.wait_ge(v_kept, t * PAIRS + max(p - 1, 0) + 1)
                for r in range(2):
                    at = (2 * p % CHUNK + r) * W
                    for k in range(KT):
                        last = nc.tensor.matmul(bank[p % 2][:, r * 3 * D:(r + 1) * 3 * D],
                                                x1[slot][:, k, at:at + W], wqkv[:, k, :],
                                                start=(k == 0), stop=(k == KT - 1))
                last.then_inc(qkv_done, 1)

            def exps_t(b, s):
                t = b * STEPS + s
                pe.wait_ge(v_exp, t + 2)
                pe.reg_add(bd_due, bd_due, 2)
                for j in range(PAIRS):
                    last = nc.tensor.transpose(pt_ps[0:D, j * P:(j + 1) * P], pr[0][:, j, :], ident[:])
                last.then_inc(pv_done, 1)

            def apply_rows(b, s):
                t = b * STEPS + s
                pe.wait_ge(bd_ready, bd_due)
                pe.wait_ge(v_stored, t + 2)
                pe.wait_ge(s_set, t + 1)
                for j in range(PAIRS):
                    last = nc.tensor.matmul(ov_ps[:, j * W:(j + 1) * W], bd[:, j, :],
                                            V[:, bass.ds(s * PAIRS + j, 1), :], start=True, stop=True)
                last.then_inc(ov_done, 1)

            def step(b, s, lag, second):
                t = b * STEPS + s
                if second and not lag:
                    for k in range(2):
                        pe.wait_ge(s_added[k], s_due[k])
                for p in range(PAIRS):
                    qkv(b, s, p)
                    if lag and p == 0:
                        exps_t(b, s - 1)
                    if lag and p == 1:
                        apply_rows(b, s - 1)
                    if second:
                        project(b - 1, s, p)
                pe.wait_ge(v_sub, t + 1)
                pe.wait_ge(qk_kept, (t + 1) * PAIRS + 1)
                for j in range(PAIRS):
                    for a in range(2):
                        row = a * PAIRS + j
                        last = nc.tensor.matmul(e_ps[a * D:(a + 1) * D, j * D:(j + 1) * D],
                                                qk_t[:, row, 0:D], qk_t[:, row, D:2 * D],
                                                start=True, stop=True)
                last.then_inc(ev_done, 1)
                pe.wait_ge(v_stored, t + 1)
                pe.wait_ge(v_kept, (t + 1) * PAIRS + 1)
                for j in range(PAIRS):
                    last = nc.tensor.transpose(vt_ps[:, j * P:(j + 1) * P], v_t[:, j, :, :], ident[:])
                last.then_inc(vt_done, 1)

            def energies(b, i, k):
                g = i * 2 + k
                pe.wait_ge(h_sub[k], b * TURNS + i + 1)
                for j in range(GPAIRS):
                    for a in range(2):
                        col = g * GW + 2 * j + a
                        last = nc.tensor.matmul(e_bank[k][a * D:(a + 1) * D, j * D:(j + 1) * D],
                                                QK[:, col, 0:D], QK[:, col, D:2 * D],
                                                start=True, stop=True)
                last.then_inc(eh_done, 1)

            def probs_t(b, i, k):
                pe.wait_ge(h_norm, b * GROUPS + i * 2 + k + 2)
                pe.reg_add(pt_due[k], pt_due[k], 2)
                for j in range(GPAIRS):
                    last = nc.tensor.transpose(pt_bank[k][0:D, j * P:(j + 1) * P], pr[k][:, j, :], ident[:])
                last.then_inc(ph_done, 1)

            def apply_cols(i, k):
                pe.wait_ge(pt_ready[k], pt_due[k])
                pe.wait_ge(s_added[k], s_due[k])
                pe.reg_add(s_due[k], s_due[k], 1)
                for w in range(GW):
                    for a in range(2):
                        half = slice(a * D, (a + 1) * D)
                        last = nc.tensor.matmul(oh_bank[k][half, w * D:(w + 1) * D], pt[k][half, w, :],
                                                V[half, :, (i * 2 + k) * GW + w], start=True, stop=True)
                last.then_inc(oh_done[k], 1)

            def middle(b, second):
                pe.wait_ge(qk_stored, (b + 1) * STEPS + 1)
                pe.wait_ge(v_kept, (b + 1) * STEPS * PAIRS + 1)
                pe.wait_ge(v_stored, (b + 1) * STEPS + 1)
                pe.wait_ge(v_sub, (b + 1) * STEPS + 1)
                for i in range(NCG // 4):
                    for q in range(4):
                        pe.wait_ge((ch_kept_dve, ch_kept_act)[q % 2], b * (NCG // 2) + max(2 * i - 1 + q // 2, 0) + 1)
                        for c in range(CG):
                            last = nc.tensor.transpose(ch_bank[q][:, c * P:(c + 1) * P],
                                                       QK[:, :, (i * 4 + q) * CG + c], ident[:])
                        last.then_inc(ch_done, 1)
                    if i == 0:
                        exps_t(b, STEPS - 1)
                    if i == 2:
                        apply_rows(b, STEPS - 1)
                    if second and i % 2:
                        project(b - 1, EARLY, i // 2)
                pe.wait_ge(ch_kept_dve, (b + 1) * (NCG // 2) + 1)
                pe.wait_ge(ch_kept_act, (b + 1) * (NCG // 2) + 1)
                pe.wait_ge(s_set, (b + 1) * STEPS + 1)
                for k in range(2):
                    energies(b, 0, k)
                for i in range(TURNS):
                    more = i + 1 < TURNS
                    units = late_units(i) if second else []
                    probs_t(b, i, 0)
                    if more:
                        energies(b, i + 1, 0)
                    for s, o in units[:1]:
                        project(b - 1, EARLY + s, o)
                    probs_t(b, i, 1)
                    apply_cols(i, 0)
                    if more:
                        energies(b, i + 1, 1)
                    for s, o in units[1:]:
                        project(b - 1, EARLY + s, o)
                    apply_cols(i, 1)

            def image(b, second):
                step(b, 0, False, second)
                if second:
                    with pe.Fori(1, EARLY) as s:
                        step(b, s, True, True)
                    with pe.Fori(EARLY, STEPS) as s:
                        step(b, s, True, False)
                else:
                    with pe.Fori(1, STEPS) as s:
                        step(b, s, True, False)
                middle(b, second)

            opened(pe, qkv_done, vt_done, ev_done, pv_done, ov_done, proj_done, ch_done, eh_done, ph_done, *oh_done)
            pe.wait_ge(weights_loaded, 16 * N_WEIGHTS)
            pe.wait_ge(ident_ready, 1)
            pe.wait_ge(consts_ready, 4)
            image(0, False)
            with pe.Fori(1, B) as b:
                image(b, True)
            with pe.Fori(0, STEPS) as s:
                for o in range(OC):
                    project(B - 1, s, o)

        @block.scalar
        def _(act):
            def load_x1(b, s, h):
                act.dma_start(x1[h][:], xk[b, :, :, bass.ds(s * (ROWS * W) + h * CHUNK * W, CHUNK * W)])\
                   .then_inc(x1_loaded[h], 16)

            def high_parts(b, s, source, at):
                t = b * STEPS + s
                for k in range(2):
                    act.wait_ge(s_added[k], (b + 1) * TURNS + 1)
                act.wait_ge(proj_done, OC * t + 1)
                for a in range(2):
                    half = slice(a * D, (a + 1) * D)
                    nc.scalar.activation(s_hl[a][half, :], source[half, bass.ds(at * PAIRS, PAIRS), :]
                                         .rearrange("p j w -> p (j w)"), ACT.Copy).then_inc(s_hi, 1)

            def diagonal(b, s):
                t = b * STEPS + s
                act.wait_ge(ov_done, t + 1)
                act.wait_ge(pv_done, t + 2)
                src = pt_ps[0:D, :].rearrange("p (j a d) -> p j a d", j=PAIRS, a=2)
                for a in range(2):
                    nc.scalar.activation(bd[a * D:(a + 1) * D, :, a * D:(a + 1) * D], src[:, :, a, :],
                                         ACT.Copy).then_inc(bd_ready, 1)

            def step(b, s, lag, second, following):
                t = b * STEPS + s
                if second:
                    high_parts(b - 1, s, S, s)
                act.wait_ge(vt_done, t + 1)
                for p in range(PAIRS):
                    act.wait_ge(qk_kept, t * PAIRS + p + 2)
                    nc.scalar.activation(v_t[:, 2 * p % PAIRS:2 * p % PAIRS + 2, 2 * p // PAIRS, :],
                                         bank[p % 2][:, 0:6 * D].rearrange("p (r d) -> p r d", r=2)[:, :, 2 * D:],
                                         ACT.Copy).then_inc(v_kept, 1)
                    if lag and p == 0:
                        diagonal(b, s - 1)
                    if following and 2 * (p + 1) % CHUNK == 0:
                        load_x1(*following, 2 * p // CHUNK)
                act.wait_ge(v_sub, t + 2)
                act.wait_ge(pv_done, t + 1)
                nc.scalar.activation(pr[0][:], es[0][:], ACT.Exp).then_inc(v_exp, 1)
                act.wait_ge(vt_done, t + 2)
                nc.scalar.activation(V[:, bass.ds(s * PAIRS, PAIRS), :],
                                     vt_ps[:].rearrange("p (j w) -> p j w", j=PAIRS),
                                     ACT.Identity, bias=bias_v[:]).then_inc(v_stored, 1)

            def exps(b, i, k):
                act.wait_ge(h_sub[k], b * TURNS + i + 2)
                nc.scalar.activation(pr[k][:], es[k][:], ACT.Exp).then_inc(h_exp, 1)

            def twice(b, i, k):
                act.wait_ge(oh_done[k], b * TURNS + i + 1)
                act.wait_ge(ph_done, b * GROUPS + i * 2 + k + 2)
                for a in range(2):
                    nc.scalar.activation(pt[k][a * D:(a + 1) * D, :, :],
                                         pt_bank[k][0:D, :].rearrange("p (w d) -> p w d", w=GW), ACT.Copy)\
                      .then_inc(pt_ready[k], 1)

            def channels(b, i, q):
                act.wait_ge(ch_done, b * NCG + i * 4 + q + 2)
                nc.scalar.activation(QK[:, :, bass.ds((i * 4 + q) * CG, CG)],
                                     ch_bank[q][:, :].rearrange("p (c w) -> p w c", c=CG),
                                     ACT.Copy).then_inc(ch_kept_act, 1)

            def middle(b, second):
                if second:
                    act.wait_ge(late_kept, b * LATE + 1)
                    high_parts(b - 1, EARLY, S_late, 0)
                for q in (1, 3):
                    channels(b, 0, q)
                diagonal(b, STEPS - 1)
                with act.Fori(1, NCG // 4) as i:
                    for q in (1, 3):
                        channels(b, i, q)
                for k in range(2):
                    exps(b, 0, k)
                if second:
                    with act.Fori(0, LATE - 1) as i2:
                        high_parts(b - 1, EARLY + 1 + i2, S_late, 1 + i2)
                        for i in range(2):
                            for k in range(2):
                                twice(b, i2 * 2 + i, k)
                                exps(b, i2 * 2 + i + 1, k)
                with act.Fori(2 * (LATE - 1) if second else 0, TURNS - 1) as i:
                    for k in range(2):
                        twice(b, i, k)
                        exps(b, i + 1, k)
                for k in range(2):
                    twice(b, TURNS - 1, k)

            def image(b, second, ahead):
                step(b, 0, False, second, (b, 1))
                if second:
                    with act.Fori(1, EARLY) as s:
                        step(b, s, True, True, (b, s + 1))
                with act.Fori(EARLY if second else 1, STEPS - 1) as s:
                    step(b, s, True, False, (b, s + 1))
                step(b, STEPS - 1, True, False, (b + 1, 0) if ahead else None)
                middle(b, second)

            for h in range(SLOTS):
                load_x1(0, 0, h)
            opened(act, v_kept, v_stored, v_exp, bd_ready, s_hi, ch_kept_act, h_exp, *pt_ready)
            act.wait_ge(weights_loaded, 16 * N_WEIGHTS)
            act.wait_ge(consts_ready, 4)
            image(0, False, True)
            with act.Fori(1, B - 1) as b:
                image(b, True, True)
            image(B - 1, True, False)
            with act.Fori(0, STEPS) as s:
                high_parts(B - 1, s, S, s)

        @block.vector
        def _(dve):
            bias2 = bias_qkv[:].unsqueeze(1).broadcast_to([P, 2, 2 * D])

            def over(v, n):
                return v[:].unsqueeze(2).broadcast_to([P, GPAIRS, n])

            def low_parts(b, s, source, at):
                t = b * STEPS + s
                for a in range(2):
                    dve.wait_ge(s_hi, 2 * t + a + 2)
                    half, other = slice(a * D, (a + 1) * D), slice((1 - a) * D, (2 - a) * D)
                    nc.vector.tensor_tensor(s_hl[a][other, :], source[half, bass.ds(at * PAIRS, PAIRS), :]
                                            .rearrange("p j w -> p (j w)"), s_hl[a][half, :].bitcast(F32),
                                            ALU.subtract).then_inc(s_lo, 1)

            def add_x(b, s, o, x_in, loaded, count):
                dve.wait_ge(loaded, count)
                dve.wait_ge(proj_done, OC * (b * STEPS + s) + o + 2)
                nc.vector.scalar_tensor_tensor(out=x_in, in0=proj_ps[:, :, :].rearrange("p a n -> p (a n)"),
                                               scalar=bias_o[:, o:o + 1], in1=x_in,
                                               op0=ALU.add, op1=ALU.add).then_inc(added, 1)

            def add_x2(b, s, o):
                add_x(b, s, o, x2[o][:], x2_loaded[o], (b * STEPS + s + 1) * 16)

            def sums_rows(b, s):
                t = b * STEPS + s
                dve.wait_ge(v_exp, t + 2)
                nc.vector.tensor_reduce(sm[0][:], pr[0][:], axis=AX.X, op=ALU.add).then_inc(v_sum, 1)
                dve.wait_ge(v_sum, t + 2)
                nc.vector.reciprocal(rs[0][:], sm[0][:]).then_inc(v_rs, 1)

            def set_s(b, s):
                t = b * STEPS + s
                dve.wait_ge(late_kept, b * LATE + 1)
                dve.wait_ge(v_rs, t + 2)
                dve.wait_ge(ov_done, t + 2)
                nc.vector.tensor_tensor(S[:, bass.ds(s * PAIRS, PAIRS), :],
                                        ov_ps[:].rearrange("p (j w) -> p j w", j=PAIRS),
                                        over(rs[0], W), ALU.mult).then_inc(s_set, 1)

            def step(b, s, lag, second):
                t = b * STEPS + s
                if second:
                    low_parts(b - 1, s, S, s)
                dve.wait_ge(ev_done, t + 1)
                dve.wait_ge(qk_stored, t + 1)
                for p in range(PAIRS):
                    dve.wait_ge(qkv_done, t * PAIRS + p + 2)
                    nc.vector.tensor_tensor(qk_t[:, 2 * p:2 * p + 2, :],
                                            bank[p % 2][:, 0:6 * D].rearrange("p (r d) -> p r d", r=2)[:, :, 0:2 * D],
                                            bias2, ALU.add).then_inc(qk_kept, 1)
                    if lag and p == 0:
                        sums_rows(b, s - 1)
                    if lag and p == 1:
                        set_s(b, s - 1)
                    if second:
                        add_x2(b - 1, s, p)
                dve.wait_ge(ev_done, t + 2)
                e = e_ps[:, 0:PAIRS * D].rearrange("p (j d) -> p j d", j=PAIRS)
                nc.vector.tensor_reduce(mx[0][:], e, axis=AX.X, op=ALU.max).then_inc(v_max, 1)
                dve.wait_ge(v_exp, t + 1)
                dve.wait_ge(v_max, t + 2)
                nc.vector.tensor_tensor(es[0][:], e, over(mx[0], D), ALU.subtract).then_inc(v_sub, 1)

            def shifted(b, i, k):
                n = b * GROUPS + i * 2 + k
                dve.wait_ge(eh_done, n + 2)
                e = e_bank[k][:, 0:GPAIRS * D].rearrange("p (j d) -> p j d", j=GPAIRS)
                nc.vector.tensor_reduce(mx[k][:], e, axis=AX.X, op=ALU.max).then_inc(h_max, 1)
                dve.wait_ge(h_max, n + 2)
                nc.vector.tensor_tensor(es[k][:], e, over(mx[k], D), ALU.subtract).then_inc(h_sub[k], 1)

            def sums_cols(b, i, k):
                n = b * GROUPS + i * 2 + k
                dve.wait_ge(h_exp, n + 2)
                nc.vector.tensor_reduce(sm[k][:], pr[k][:], axis=AX.X, op=ALU.add).then_inc(h_sum, 1)
                dve.wait_ge(h_sum, n + 2)
                nc.vector.reciprocal(rs[k][:], sm[k][:]).then_inc(h_rs, 1)

            def add_s(b, i, k):
                dve.wait_ge(oh_done[k], b * TURNS + i + 2)
                cols = S[:, :, bass.ds((i * 2 + k) * GW, GW)]
                nc.vector.tensor_tensor(cols, oh_bank[k][:].rearrange("p (w j) -> p j w", w=GW), cols,
                                        ALU.add).then_inc(s_added[k], 1)

            def channels(b, i, q):
                dve.wait_ge(ch_done, b * NCG + i * 4 + q + 2)
                nc.vector.tensor_copy(QK[:, :, bass.ds((i * 4 + q) * CG, CG)],
                                      ch_bank[q][:, :].rearrange("p (c w) -> p w c", c=CG)).then_inc(ch_kept_dve, 1)

            def turn(b, i, units):
                for k in range(2):
                    shifted(b, i + 1, k)
                    for s, o in units[k:k + 1]:
                        add_x2(b - 1, s, o)
                    add_s(b, i, k)
                    sums_cols(b, i + 1, k)

            def middle(b, second):
                if second:
                    low_parts(b - 1, EARLY, S_late, 0)
                for q in (0, 2):
                    channels(b, 0, q)
                sums_rows(b, STEPS - 1)
                for i in range(1, 3):
                    for q in (0, 2):
                        channels(b, i, q)
                    if second and i % 2:
                        add_x2(b - 1, EARLY, i // 2)
                set_s(b, STEPS - 1)
                for i in range(3, NCG // 4):
                    for q in (0, 2):
                        channels(b, i, q)
                    if second and i % 2:
                        add_x2(b - 1, EARLY, i // 2)
                dve.wait_ge(s_set, (b + 1) * STEPS + 1)
                for k in range(2):
                    shifted(b, 0, k)
                for k in range(2):
                    sums_cols(b, 0, k)
                if second:
                    with dve.Fori(0, LATE - 1) as i2:
                        s = EARLY + 1 + i2
                        low_parts(b - 1, s, S_late, 1 + i2)
                        turn(b, i2 * 2, [(s, 0), (s, 1)])
                        turn(b, i2 * 2 + 1, [(s, 2), (s, 3)])
                with dve.Fori(2 * (LATE - 1) if second else 0, TURNS - 1) as i:
                    turn(b, i, [])
                for k in range(2):
                    add_s(b, TURNS - 1, k)

            def image(b, second):
                step(b, 0, False, second)
                if second:
                    with dve.Fori(1, EARLY) as s:
                        step(b, s, True, True)
                with dve.Fori(EARLY if second else 1, STEPS) as s:
                    step(b, s, True, False)
                middle(b, second)

            opened(dve, qk_kept, v_max, v_sub, v_sum, v_rs, s_set, s_lo, added, ch_kept_dve,
                   h_max, h_sum, h_rs, *h_sub, *s_added)
            nc.vector.memset(bd[:], 0.0).then_inc(consts_ready, 1)
            dve.wait_ge(weights_loaded, 16 * N_WEIGHTS)
            nc.vector.tensor_scalar(wo_raw, wo_raw, gam[:], None, ALU.mult).then_inc(consts_ready, 1)
            dve.wait_ge(consts_ready, 2)
            nc.vector.tensor_copy(wo_hi[:], wo_raw).then_inc(consts_ready, 1)
            dve.wait_ge(consts_ready, 3)
            nc.vector.tensor_tensor(wo_lo[:], wo_raw, wo_hi[:].bitcast(F32), ALU.subtract).then_inc(consts_ready, 1)
            dve.wait_ge(consts_ready, 4)
            image(0, False)
            with dve.Fori(1, B) as b:
                image(b, True)
            with dve.Fori(0, STEPS // SETS) as r:
                for n in range(SETS):
                    s = r * SETS + n
                    low_parts(B - 1, s, S, s)
                    for o in range(OC):
                        add_x(B - 1, s, o, x_end[n][o], end_loaded[n][o], 16 * (r + 1))


def kernel(x, L0_conv_qkv_w, L0_conv_qkv_b, L0_conv_out_w, L0_conv_out_b, L0_conv_gamma):
    import numpy as np
    import concourse.bacc as bacc
    from concourse.bass_utils import run_bass_kernel_spmd

    arrays = {
        "x": np.ascontiguousarray(x),
        "wqkv_t": np.ascontiguousarray(np.asarray(L0_conv_qkv_w).T),
        "qkv_b": np.ascontiguousarray(L0_conv_qkv_b),
        "wo_t": np.ascontiguousarray(np.asarray(L0_conv_out_w).T),
        "out_b": np.ascontiguousarray(np.asarray(L0_conv_out_b).reshape(OC, P).T),
        "gamma": np.ascontiguousarray(L0_conv_gamma).reshape(1),
    }
    nc = bacc.Bacc("TRN2", target_bir_lowering=False, num_devices=1)
    aps = [nc.dram_tensor(n, a.shape, mybir.dt.from_np(a.dtype), kind="ExternalInput").ap() for n, a in arrays.items()]
    out = nc.dram_tensor("out", (B, C, H, W), F32, kind="ExternalOutput").ap()
    axial_attention(nc, *aps, out)
    r = run_bass_kernel_spmd(nc, [arrays], core_ids=[0])
    return r.results[0]["out"]
```

```python
from contextlib import ExitStack

import concourse.bass as bass
from concourse import mybir
from concourse.alu_op_type import AluOpType as ALU

F32 = mybir.dt.float32
F32R = mybir.dt.float32r
ACT = mybir.ActivationFunctionType
AX = mybir.AxisListType

B, C, H, W = 8, 512, 128, 128
D = C // 8
P = 128
KT = C // P
OC = C // P
ROWS = 8
STEPS = H // ROWS
PAIRS = ROWS // 2
CHUNK = 4
SLOTS = ROWS // CHUNK
ROUND = 4
BESIDE = 3
EARLY = STEPS // ROUND * BESIDE
LATE = STEPS - EARLY
KEPT = STEPS - BESIDE
CG = 4
NCG = 2 * D // CG
EARLY_AT = (3, 5, 7)
GW = 8
GROUPS = W // GW
TURNS = GROUPS // 2
GPAIRS = GW // 2
SETS = 6
OPEN_PROJ = OC + 1
N_WEIGHTS = 7


def axial_attention(nc, x, wqkv_t, qkv_b, wo_t, out_b, gamma, out):
    xk = x.rearrange("b (t p) h w -> b p t (h w)", p=P)
    xo = x.rearrange("b (t p) h w -> b t p (h w)", p=P)
    yo = out.rearrange("b (t p) h w -> b t p (h w)", p=P)

    with ExitStack() as ctx:
        def sb(name, shape, dtype=F32):
            return ctx.enter_context(nc.sbuf_tensor(name, shape, dtype))

        def sem(name):
            return ctx.enter_context(nc.semaphore(name))

        wqkv = sb("wqkv", [P, KT, 3 * D])
        bias_qkv = sb("bias_qkv", [P, 2 * D])
        bias_v = sb("bias_v", [P, 1])
        wo_hi = sb("wo_hi", [P, C], F32R)
        wo_lo = sb("wo_lo", [P, C], F32R)
        bias_o = sb("bias_o", [P, OC])
        gam = sb("gam", [P, 1])
        ident = sb("ident", [P, P])
        QK = sb("QK", [P, 2, H, D])
        V = sb("V", [P, H // 2, W])
        S = sb("S", [P, H // 2, W])
        S_late = sb("S_late", [P, LATE * PAIRS, W])
        x1 = [sb(f"x1_{i}", [P, KT, CHUNK * W]) for i in range(SLOTS)]
        x2 = [sb(f"x2_{o}", [P, ROWS * W]) for o in range(OC)]
        x_end = [[x2[o][:] for o in range(OC)],
                 [x1[o // 2][:].rearrange("p k n -> p (k n)")[:, o % 2 * ROWS * W:(o % 2 + 1) * ROWS * W]
                  for o in range(OC)]]
        x_end += [[QK[:].rearrange("p q r d -> p (q r d)")[:, (n * OC + o) * ROWS * W:(n * OC + o + 1) * ROWS * W]
                   for o in range(OC)] for n in range(SETS - 2)]
        qk_t = sb("qk_t", [P, 2, PAIRS, 2, D])
        s_hl = sb("s_hl", [P, 2, 2, PAIRS * W], F32R)
        v_t = sb("v_t", [P, PAIRS, 2, D])
        es = [sb(f"es{i}", [P, GPAIRS, D]) for i in range(2)]
        pr = [sb(f"pr{i}", [P, GPAIRS, D]) for i in range(2)]
        mx = [sb(f"mx{i}", [P, GPAIRS]) for i in range(2)]
        sm = [sb(f"sm{i}", [P, GPAIRS]) for i in range(2)]
        rs = [sb(f"rs{i}", [P, GPAIRS]) for i in range(2)]
        bd = sb("bd", [P, PAIRS, 2 * D])
        pt = [sb(f"pt{i}", [P, GW, D]) for i in range(2)]
        wo_raw = qk_t[:, 0, :, :, :].rearrange("p j a d -> p (j a d)")

        psum = ctx.enter_context(nc.psum_tensor("psum", [P, 8, 512], F32))
        bank = [psum[:, i, :] for i in range(8)]
        proj_ps, proj_ps2 = psum[:, 2:4, :], psum[:, 4:6, :]
        vt_ps, e_ps, pt_ps, ov_ps = bank[4:8]
        ch_bank = (bank[0], bank[1], bank[4], bank[5])
        e_bank, pt_bank, oh_bank = (bank[5], bank[4]), (bank[6], bank[0]), (bank[7], bank[1])

        wqkv_loaded = sem("wqkv_loaded")
        weights_loaded = sem("weights_loaded")
        ident_zero = sem("ident_zero")
        ident_ready = sem("ident_ready")
        consts_ready = sem("consts_ready")
        x1_loaded = [sem(f"x1_loaded{i}") for i in range(SLOTS)]
        x2_loaded = [sem(f"x2_loaded{o}") for o in range(OC)]
        stored = [sem(f"stored{o}") for o in range(OC)]
        end_loaded = [x2_loaded] + [[sem(f"end_loaded{n}_{o}") for o in range(OC)] for n in range(1, SETS)]
        end_stored = [stored] + [[sem(f"end_stored{n}_{o}") for o in range(OC)] for n in range(1, SETS)]
        qkv_done = sem("qkv_done")
        qk_kept = sem("qk_kept")
        qk_stored = sem("qk_stored")
        v_kept = sem("v_kept")
        vt_done = sem("vt_done")
        v_stored = sem("v_stored")
        ev_done = sem("ev_done")
        v_max = sem("v_max")
        v_sub = sem("v_sub")
        v_exp = sem("v_exp")
        v_sum = sem("v_sum")
        v_rs = sem("v_rs")
        pv_done = sem("pv_done")
        bd_ready = sem("bd_ready")
        ov_done = sem("ov_done")
        s_set = sem("s_set")
        late_kept = sem("late_kept")
        s_hi = sem("s_hi")
        s_lo = sem("s_lo")
        proj_done = sem("proj_done")
        added = sem("added")
        ch_done = sem("ch_done")
        ch_kept_dve = sem("ch_kept_dve")
        ch_kept_act = sem("ch_kept_act")
        eh_done = sem("eh_done")
        h_max = sem("h_max")
        h_sub = [sem(f"h_sub{i}") for i in range(2)]
        h_exp = sem("h_exp")
        h_sum = sem("h_sum")
        h_rs = sem("h_rs")
        h_norm = sem("h_norm")
        ph_done = sem("ph_done")
        pt_ready = [sem(f"pt_ready{i}") for i in range(2)]
        oh_done = [sem(f"oh_done{i}") for i in range(2)]
        s_added = [sem(f"s_added{i}") for i in range(2)]

        def later(n):
            return not isinstance(n, int) or n > 0

        def loads(n, count):
            return 16 * (count + (0 if n else (B - 1) * STEPS))

        def stores(n, count):
            return loads(n, count) + (0 if n else 1)

        def opened(engine, *sems):
            for one in sems:
                engine.sem_inc(one, 1)

        def late_units(i):
            return [(1 + i // 2, 2 * (i % 2) + o) for o in range(2)] if i // 2 + 1 < LATE else []

        def channels_of(i, q):
            per = D // CG // 4
            return QK[:, bass.ds(i // per, 1), :, bass.ds((i % per) * 4 * CG + q * CG, CG)]\
                .rearrange("p o w c -> p (o w) c")

        def source(s):
            if isinstance(s, int) and s < BESIDE:
                return S, s
            return S_late, s & (LATE - 1)

        block = ctx.enter_context(nc.Block())

        @block.sync
        def _(sp):
            sp.dma_start(wqkv[:], wqkv_t.rearrange("(t p) o -> p t o", p=P)).then_inc(wqkv_loaded, 16)
            sp.dma_start(bias_qkv[:], qkv_b[0:2 * D].partition_broadcast(P)).then_inc(weights_loaded, 16)
            bv = qkv_b[2 * D:3 * D].rearrange("(d o) -> d o", o=1)
            for a in range(2):
                sp.dma_start(bias_v[a * D:(a + 1) * D, :], bv).then_inc(weights_loaded, 16)
                sp.dma_start(wo_raw[a * D:(a + 1) * D, :], wo_t).then_inc(weights_loaded, 16)
            sp.dma_start(bias_o[:], out_b).then_inc(weights_loaded, 16)
            sp.dma_start(gam[:], gamma.partition_broadcast(P)).then_inc(weights_loaded, 16)
            opened(sp, *stored)

            def load(b, s, o, t):
                sp.wait_ge(stored[o], 16 * t + 1)
                sp.dma_start(x2[o][:], xo[b, o, :, bass.ds(s * (ROWS * W), ROWS * W)]).then_inc(x2_loaded[o], 16)

            def step(b, s, following):
                t = b * STEPS + s
                for o in range(OC):
                    sp.wait_ge(added, OC * t + o + 2)
                    sp.dma_start(yo[b, o, :, bass.ds(s * (ROWS * W), ROWS * W)], x2[o][:]).then_inc(stored[o], 16)
                    if o > 0:
                        load(*following, o - 1, t + 1)
                load(*following, OC - 1, t + 1)

            for o in range(OC):
                load(0, 0, o, 0)
            with sp.Fori(0, B - 1) as b:
                with sp.Fori(0, STEPS - 1) as s:
                    step(b, s, (b, s + 1))
                step(b, STEPS - 1, (b + 1, 0))

            def load_end(s):
                for o in range(OC):
                    n = s % SETS
                    if s >= SETS:
                        sp.wait_ge(end_stored[n][o], stores(n, s // SETS))
                    sp.dma_start(x_end[n][o], xo[B - 1, o, :, s * ROWS * W:(s + 1) * ROWS * W])\
                      .then_inc(end_loaded[n][o], 16)

            sp.wait_ge(qkv_done, B * STEPS * PAIRS + 1)
            load_end(1)
            sp.wait_ge(eh_done, B * GROUPS + 1)
            for s in range(2, SETS):
                load_end(s)
            for s in range(STEPS):
                for o in range(OC):
                    sp.wait_ge(added, OC * ((B - 1) * STEPS + s) + o + 2)
                    sp.dma_start(yo[B - 1, o, :, s * ROWS * W:(s + 1) * ROWS * W], x_end[s % SETS][o])\
                      .then_inc(end_stored[s % SETS][o], 16)
                if s + SETS < STEPS:
                    load_end(s + SETS)
            for n in range(SETS):
                for o in range(OC):
                    sp.wait_ge(end_stored[n][o], stores(n, STEPS // SETS + (n < STEPS % SETS)))

        @block.gpsimd
        def _(pool):
            nc.gpsimd.memset(ident[:], 0.0).then_inc(ident_zero, 1)
            pool.wait_ge(ident_zero, 1)
            nc.gpsimd.affine_select(out=ident[:], in_=ident[:], compare_op=ALU.not_equal, fill=1.0, base=0,
                                    pattern=[[-1, P]], channel_multiplier=1).then_inc(ident_ready, 1)
            opened(pool, qk_stored, late_kept, h_norm, s_lo)
            qk_due, split_due = pool.alloc_register("qk_due"), pool.alloc_register("split_due")
            pool.reg_mov(qk_due, PAIRS + 1)
            pool.reg_mov(split_due, 1)
            low_due = pool.alloc_register("low_due")
            pool.reg_mov(low_due, 2)

            def copy_qk(b, s):
                pool.wait_ge(qk_kept, qk_due)
                pool.reg_add(qk_due, qk_due, PAIRS)
                for q in range(2):
                    nc.gpsimd.tensor_copy(QK[:, q, bass.ds(s * ROWS, ROWS), :],
                                          qk_t[:, q].rearrange("p j a d -> p (j a) d")).then_inc(qk_stored, 1)

            def copy_s(b, s):
                for k in range(2):
                    pool.wait_ge(s_added[k], b * TURNS + 1)
                pool.wait_ge(s_lo, split_due)
                pool.reg_add(split_due, split_due, 2)
                nc.gpsimd.tensor_copy(S_late[:, bass.ds((s & (LATE - 1)) * PAIRS, PAIRS), :],
                                      S[:, bass.ds(s * PAIRS, PAIRS), :]).then_inc(late_kept, 1)

            def low_part(b, s, held, at, a, own, count):
                t = b * STEPS + s
                pool.wait_ge(own, count)
                pool.wait_ge(s_hi, 2 * t + a + 2)
                half, other = slice(a * D, (a + 1) * D), slice((1 - a) * D, (2 - a) * D)
                parts = s_hl[:, bass.ds(t & 1, 1), a, :].rearrange("p o n -> p (o n)")
                nc.gpsimd.tensor_tensor(parts[other, :], held[half, bass.ds(at * PAIRS, PAIRS), :]
                                        .rearrange("p j w -> p (j w)"), parts[half, :].bitcast(F32),
                                        ALU.subtract).then_inc(s_lo, 1)
                pool.wait_ge(s_lo, low_due)
                pool.reg_add(low_due, low_due, 1)

            def low_parts(b, s, held, at, own, count):
                for a in range(2):
                    low_part(b, s, held, at, a, own, count)

            def round_of_steps(b, r):
                for u in range(ROUND):
                    s = r * ROUND + u
                    copy_s(b, s)
                    if u < BESIDE:
                        low_parts(b - 1, r * BESIDE + u, *source(r * BESIDE + u),
                                  late_kept, (b - 1) * KEPT + s - BESIDE + 2)
                    copy_qk(b, s)

            def normed(b, i, split=None):
                for k in range(2):
                    pool.wait_ge(h_rs, b * GROUPS + i * 2 + k + 2)
                    nc.gpsimd.tensor_tensor(pr[k][:], pr[k][:],
                                            rs[k][:].unsqueeze(2).broadcast_to([P, GPAIRS, D]),
                                            ALU.mult).then_inc(h_norm, 1)
                    if split:
                        low_part(b - 1, split[0], S_late, split[1], k, h_norm, b * GROUPS + i * 2 + k + 2)

            def image(b, second):
                if second:
                    with pool.Fori(0, BESIDE) as s:
                        pool.wait_ge(h_norm, b * GROUPS + 1)
                        low_parts(b - 1, s, S, s, qk_stored, 2 * (b * STEPS + s) + 1)
                        copy_qk(b, s)
                    with pool.Fori(BESIDE, ROUND) as s:
                        copy_s(b, s)
                        copy_qk(b, s)
                    with pool.Fori(1, STEPS // ROUND) as r:
                        round_of_steps(b, r)
                    pool.reg_add(split_due, split_due, 2 * BESIDE)
                    for n in range(2):
                        low_parts(b - 1, EARLY + n, S_late, n, qk_stored, 2 * (b + 1) * STEPS + 1)
                    with pool.Fori(0, LATE - 2) as i2:
                        normed(b, 2 * i2)
                        normed(b, 2 * i2 + 1, (EARLY + 2 + i2, i2 + 2))
                else:
                    with pool.Fori(0, STEPS) as s:
                        copy_qk(b, s)
                with pool.Fori(2 * (LATE - 2) if second else 0, TURNS) as i:
                    normed(b, i)

            image(0, False)
            with pool.Fori(1, B) as b:
                image(b, True)
            with pool.Fori(0, STEPS) as s:
                low_parts(B - 1, s, S, s, h_norm, B * GROUPS + 1)

        @block.tensor
        def _(pe):
            bd_due = pe.alloc_register("bd_due")
            pt_due = [pe.alloc_register(f"pt_due{k}") for k in range(2)]
            s_due = [pe.alloc_register(f"s_due{k}") for k in range(2)]
            for due in (bd_due, *pt_due, *s_due):
                pe.reg_mov(due, 1)

            def project(b, s, o, end=False):
                t = b * STEPS + s
                if o == 0:
                    pe.wait_ge(s_lo, 2 * t + 3)
                to = proj_ps2 if end and o % 2 else proj_ps
                pe.wait_ge(added, OC * t + o + (0 if end else 1))
                for a in range(2):
                    for k, w in enumerate((wo_hi, wo_lo)):
                        last = nc.tensor.matmul(to[:, a, :], w[:, o * P:(o + 1) * P],
                                                s_hl[:, bass.ds(t & 1, 1), a, :],
                                                start=(k == 0), stop=(k == 1))
                last.then_inc(proj_done, 1)

            def qkv(b, s, p):
                t = b * STEPS + s
                slot = 2 * p // CHUNK
                if 2 * p % CHUNK == 0:
                    pe.wait_ge(x1_loaded[slot], (t + 1) * 16)
                pe.wait_ge(v_kept, t * PAIRS + max(p - 1, 0) + 1)
                for r in range(2):
                    at = (2 * p % CHUNK + r) * W
                    for k in range(KT):
                        last = nc.tensor.matmul(bank[p % 2][:, r * 3 * D:(r + 1) * 3 * D],
                                                x1[slot][:, k, at:at + W], wqkv[:, k, :],
                                                start=(k == 0), stop=(k == KT - 1))
                last.then_inc(qkv_done, 1)

            def exps_t(b, s):
                t = b * STEPS + s
                pe.wait_ge(v_exp, t + 2)
                pe.reg_add(bd_due, bd_due, 2)
                for j in range(PAIRS):
                    last = nc.tensor.transpose(pt_ps[0:D, j * P:(j + 1) * P], pr[0][:, j, :], ident[:])
                last.then_inc(pv_done, 1)

            def apply_rows(b, s):
                t = b * STEPS + s
                pe.wait_ge(bd_ready, bd_due)
                pe.wait_ge(v_stored, t + 2)
                pe.wait_ge(s_set, t + 1)
                for j in range(PAIRS):
                    last = nc.tensor.matmul(ov_ps[:, j * W:(j + 1) * W], bd[:, j, :],
                                            V[:, bass.ds(s * PAIRS + j, 1), :], start=True, stop=True)
                last.then_inc(ov_done, 1)

            def step(b, s, lag, beside):
                t = b * STEPS + s
                for p in range(PAIRS):
                    if later(b) and not lag and p == 1:
                        for k in range(2):
                            pe.wait_ge(s_added[k], s_due[k])
                    qkv(b, s, p)
                    if lag and p == 0:
                        exps_t(b, s - 1)
                    if lag and p == 1:
                        apply_rows(b, s - 1)
                    if beside is not None:
                        project(b - 1, beside, p)
                if not later(b) and not lag:
                    pe.wait_ge(ident_ready, 1)
                pe.wait_ge(v_sub, 2 * t + 1)
                pe.wait_ge(v_stored, t + 1)
                for n in range(2):
                    pe.wait_ge(qk_kept, t * PAIRS + PAIRS // 2 + n + 2)
                    for j in range(2 * n, 2 * n + 2):
                        last = nc.tensor.matmul(e_ps[:, j * P:(j + 1) * P], qk_t[:, 0, j, :, :], qk_t[:, 1, j, :, :],
                                                start=True, stop=True)
                    if n == 1:
                        last.then_inc(ev_done, 1)
                    pe.wait_ge(v_kept, t * PAIRS + PAIRS // 2 + n + 2)
                    for j in range(2 * n, 2 * n + 2):
                        last = nc.tensor.transpose(vt_ps[:, j * P:(j + 1) * P], v_t[:, j, :, :], ident[:])
                last.then_inc(vt_done, 1)

            def round_of_steps(b, r):
                for u in range(ROUND):
                    step(b, r * ROUND + u, u > 0 or later(r), r * BESIDE + u - 1 if u > 0 else None)

            def energies(b, i, k):
                g = i * 2 + k
                pe.wait_ge(h_sub[k], 2 * (b * TURNS + i) + 1)
                for j in range(GPAIRS):
                    cols = slice(g * GW + 2 * j, g * GW + 2 * j + 2)
                    last = nc.tensor.matmul(e_bank[k][:, j * P:(j + 1) * P], QK[:, 0, cols, :], QK[:, 1, cols, :],
                                            start=True, stop=True)
                last.then_inc(eh_done, 1)

            def probs_t(b, i, k):
                pe.wait_ge(h_norm, b * GROUPS + i * 2 + k + 2)
                pe.reg_add(pt_due[k], pt_due[k], 2)
                for j in range(GPAIRS):
                    last = nc.tensor.transpose(pt_bank[k][0:D, j * P:(j + 1) * P], pr[k][:, j, :], ident[:])
                last.then_inc(ph_done, 1)

            def apply_cols(i, k):
                pe.wait_ge(pt_ready[k], pt_due[k])
                pe.wait_ge(s_added[k], s_due[k])
                pe.reg_add(s_due[k], s_due[k], 1)
                for w in range(GW):
                    for a in range(2):
                        half = slice(a * D, (a + 1) * D)
                        last = nc.tensor.matmul(oh_bank[k][half, w * D:(w + 1) * D], pt[k][half, w, :],
                                                V[half, :, (i * 2 + k) * GW + w], start=True, stop=True)
                last.then_inc(oh_done[k], 1)

            def middle(b, second):
                if not second:
                    pe.wait_ge(consts_ready, 4)
                pe.wait_ge(qk_stored, 2 * (b + 1) * STEPS)
                pe.wait_ge(v_kept, (b + 1) * STEPS * PAIRS + 1)
                for i in range(NCG // 4):
                    if i == NCG // 8:
                        pe.wait_ge(qk_stored, 2 * (b + 1) * STEPS + 1)
                    for q in range(4):
                        if i == 0 and q == 2:
                            pe.wait_ge(v_stored, (b + 1) * STEPS + 1)
                        if i == 0 and q == 3:
                            pe.wait_ge(v_sub, 2 * (b + 1) * STEPS + 1)
                        pe.wait_ge((ch_kept_dve, ch_kept_act)[q % 2], b * (NCG // 2) + max(2 * i - 1 + q // 2, 0) + 1)
                        for c in range(CG):
                            ch = (i * 4 + q) * CG + c
                            last = nc.tensor.transpose(ch_bank[q][:, c * P:(c + 1) * P],
                                                       QK[:, ch // D, :, ch % D], ident[:])
                        last.then_inc(ch_done, 1)
                    if i == 0:
                        exps_t(b, STEPS - 1)
                    if i == 1:
                        apply_rows(b, STEPS - 1)
                    if second and i in EARLY_AT:
                        project(b - 1, EARLY, EARLY_AT.index(i))
                pe.wait_ge(ch_kept_dve, (b + 1) * (NCG // 2) + 1)
                pe.wait_ge(ch_kept_act, (b + 1) * (NCG // 2) + 1)
                pe.wait_ge(s_set, (b + 1) * STEPS + 1)
                for k in range(2):
                    energies(b, 0, k)
                if second:
                    project(b - 1, EARLY, 3)
                for i in range(TURNS):
                    more = i + 1 < TURNS
                    units = late_units(i) if second else []
                    probs_t(b, i, 0)
                    if more:
                        energies(b, i + 1, 0)
                    for s, o in units[:1]:
                        project(b - 1, EARLY + s, o)
                    probs_t(b, i, 1)
                    apply_cols(i, 0)
                    if more:
                        energies(b, i + 1, 1)
                    for s, o in units[1:]:
                        project(b - 1, EARLY + s, o)
                    apply_cols(i, 1)

            def image(b, second):
                if second:
                    round_of_steps(b, 0)
                    with pe.Fori(1, STEPS // ROUND) as r:
                        round_of_steps(b, r)
                else:
                    step(b, 0, False, None)
                    with pe.Fori(1, STEPS) as s:
                        step(b, s, True, None)
                middle(b, second)

            opened(pe, qkv_done, vt_done, ev_done, pv_done, ov_done, ch_done, eh_done, ph_done, *oh_done)
            pe.sem_inc(proj_done, OPEN_PROJ)
            pe.wait_ge(wqkv_loaded, 16)
            image(0, False)
            with pe.Fori(1, B) as b:
                image(b, True)
            with pe.Fori(0, STEPS) as s:
                for o in range(OC):
                    project(B - 1, s, o, True)

        @block.scalar
        def _(act):
            def load_x1(b, s, h):
                act.dma_start(x1[h][:], xk[b, :, :, bass.ds(s * (ROWS * W) + h * CHUNK * W, CHUNK * W)])\
                   .then_inc(x1_loaded[h], 16)

            def high_parts(b, s, held, at, row_halves=(0, 1)):
                t = b * STEPS + s
                if held is S:
                    for k in range(2):
                        act.wait_ge(s_added[k], (b + 1) * TURNS + 1)
                else:
                    act.wait_ge(late_kept, b * KEPT + s - BESIDE + 2)
                act.wait_ge(proj_done, OC * (t - 1) + OPEN_PROJ)
                for a in row_halves:
                    half = slice(a * D, (a + 1) * D)
                    nc.scalar.activation(s_hl[half, bass.ds(t & 1, 1), a, :].rearrange("p o n -> p (o n)"),
                                         held[half, bass.ds(at * PAIRS, PAIRS), :]
                                         .rearrange("p j w -> p (j w)"), ACT.Copy).then_inc(s_hi, 1)

            def diagonal(b, s):
                t = b * STEPS + s
                act.wait_ge(ov_done, t + 1)
                act.wait_ge(pv_done, t + 2)
                src = pt_ps[0:D, :].rearrange("p (j a d) -> p j a d", j=PAIRS, a=2)
                for a in range(2):
                    nc.scalar.activation(bd[a * D:(a + 1) * D, :, a * D:(a + 1) * D], src[:, :, a, :],
                                         ACT.Copy).then_inc(bd_ready, 1)

            def step(b, s, lag, split, following):
                t = b * STEPS + s
                act.wait_ge(vt_done, t + 1)
                for p in range(PAIRS):
                    act.wait_ge(qk_kept, t * PAIRS + p + 2)
                    nc.scalar.activation(v_t[:, 2 * p % PAIRS:2 * p % PAIRS + 2, 2 * p // PAIRS, :],
                                         bank[p % 2][:, 0:6 * D].rearrange("p (r d) -> p r d", r=2)[:, :, 2 * D:],
                                         ACT.Copy).then_inc(v_kept, 1)
                    if lag and p == 0:
                        diagonal(b, s - 1)
                    if following and 2 * (p + 1) % CHUNK == 0:
                        load_x1(*following, 2 * p // CHUNK)
                    if split is not None and p == 1:
                        high_parts(b - 1, split, *source(split))
                act.wait_ge(vt_done, t + 2)
                nc.scalar.activation(V[:, bass.ds(s * PAIRS, PAIRS), :],
                                     vt_ps[:].rearrange("p (j w) -> p j w", j=PAIRS),
                                     ACT.Identity, bias=bias_v[:]).then_inc(v_stored, 1)
                act.wait_ge(v_sub, 2 * t + 3)
                act.wait_ge(pv_done, t + 1)
                nc.scalar.activation(pr[0][:], es[0][:], ACT.Exp).then_inc(v_exp, 1)

            def exps(b, i, k):
                act.wait_ge(h_sub[k], 2 * (b * TURNS + i) + 3)
                nc.scalar.activation(pr[k][:], es[k][:], ACT.Exp).then_inc(h_exp, 1)

            def twice(b, i, k):
                act.wait_ge(oh_done[k], b * TURNS + i + 1)
                act.wait_ge(ph_done, b * GROUPS + i * 2 + k + 2)
                for a in range(2):
                    nc.scalar.activation(pt[k][a * D:(a + 1) * D, :, :],
                                         pt_bank[k][0:D, :].rearrange("p (w d) -> p w d", w=GW), ACT.Copy)\
                      .then_inc(pt_ready[k], 1)

            def channels(b, i, q):
                act.wait_ge(ch_done, b * NCG + i * 4 + q + 2)
                nc.scalar.activation(channels_of(i, q), ch_bank[q].rearrange("p (c w) -> p w c", c=CG),
                                     ACT.Copy).then_inc(ch_kept_act, 1)

            def middle(b, second):
                for q in (1, 3):
                    channels(b, 0, q)
                diagonal(b, STEPS - 1)
                for n in range(2):
                    if second:
                        high_parts(b - 1, EARLY + n, S_late, n)
                    with act.Fori(1 + 2 * n, 3 if n == 0 else NCG // 4) as i:
                        for q in (1, 3):
                            channels(b, i, q)
                for k in range(2):
                    exps(b, 0, k)
                if second:
                    with act.Fori(0, LATE - 2) as i2:
                        for i in range(2):
                            for k in range(2):
                                twice(b, i2 * 2 + i, k)
                                exps(b, i2 * 2 + i + 1, k)
                                if i == 0:
                                    high_parts(b - 1, EARLY + 2 + i2, S_late, i2 + 2, (k,))
                with act.Fori(2 * (LATE - 2) if second else 0, TURNS - 1) as i:
                    for k in range(2):
                        twice(b, i, k)
                        exps(b, i + 1, k)
                for k in range(2):
                    twice(b, TURNS - 1, k)

            def round_of_steps(b, r, after):
                for u in range(ROUND):
                    s = r * ROUND + u
                    step(b, s, u > 0 or later(r), r * BESIDE + u if u < BESIDE else None,
                         (b, s + 1) if u < ROUND - 1 else after)

            def image(b, second, ahead):
                after = (b + 1, 0) if ahead else None
                if second:
                    last_r = STEPS // ROUND - 1
                    round_of_steps(b, 0, (b, ROUND))
                    with act.Fori(1, last_r) as r:
                        round_of_steps(b, r, (b, (r + 1) * ROUND))
                    round_of_steps(b, last_r, after)
                else:
                    step(b, 0, False, None, (b, 1))
                    with act.Fori(1, STEPS - 1) as s:
                        step(b, s, True, None, (b, s + 1))
                    step(b, STEPS - 1, True, None, after)
                middle(b, second)

            for h in range(SLOTS):
                load_x1(0, 0, h)
            opened(act, v_kept, v_stored, v_exp, bd_ready, s_hi, ch_kept_act, h_exp, *pt_ready)
            act.wait_ge(weights_loaded, 16 * N_WEIGHTS)
            act.wait_ge(consts_ready, 4)
            image(0, False, True)
            with act.Fori(1, B - 1) as b:
                image(b, True, True)
            image(B - 1, True, False)
            with act.Fori(0, STEPS) as s:
                high_parts(B - 1, s, S, s)

        @block.vector
        def _(dve):
            bias2 = bias_qkv[:].rearrange("p (q d) -> p q d", q=2).unsqueeze(2).broadcast_to([P, 2, 2, D])

            halves = (slice(0, D), slice(D, P))

            def own(energies, a):
                return energies.rearrange("p (j d) -> p j d", d=P)[halves[a], :, halves[a]]

            def over(v, n):
                return v[:].unsqueeze(2).broadcast_to([P, GPAIRS, n])

            def add_x(b, s, o, x_in, loaded, count, ps=proj_ps):
                dve.wait_ge(loaded, count)
                dve.wait_ge(proj_done, OC * (b * STEPS + s) + o + 1 + OPEN_PROJ)
                nc.vector.scalar_tensor_tensor(out=x_in, in0=ps.rearrange("p a n -> p (a n)"),
                                               scalar=bias_o[:, o:o + 1], in1=x_in,
                                               op0=ALU.add, op1=ALU.add).then_inc(added, 1)

            def add_x2(b, s, o):
                add_x(b, s, o, x2[o][:], x2_loaded[o], (b * STEPS + s + 1) * 16)

            def sums_rows(b, s):
                t = b * STEPS + s
                dve.wait_ge(v_exp, t + 2)
                nc.vector.tensor_reduce(sm[0][:], pr[0][:], axis=AX.X, op=ALU.add).then_inc(v_sum, 1)
                dve.wait_ge(v_sum, t + 2)
                nc.vector.reciprocal(rs[0][:], sm[0][:]).then_inc(v_rs, 1)

            def set_s(b, s, kept=None):
                t = b * STEPS + s
                if kept is not None:
                    dve.wait_ge(late_kept, kept + 1)
                dve.wait_ge(v_rs, t + 2)
                dve.wait_ge(ov_done, t + 2)
                nc.vector.tensor_tensor(S[:, bass.ds(s * PAIRS, PAIRS), :],
                                        ov_ps[:].rearrange("p (j w) -> p j w", j=PAIRS),
                                        over(rs[0], W), ALU.mult).then_inc(s_set, 1)

            def step(b, s, lag, beside, kept=None):
                t = b * STEPS + s
                dve.wait_ge(ev_done, t + 1)
                dve.wait_ge(qk_stored, 2 * t + 1)
                for p in range(PAIRS):
                    dve.wait_ge(qkv_done, t * PAIRS + p + 2)
                    j = 2 * p % PAIRS
                    nc.vector.tensor_tensor(qk_t[:, :, j:j + 2, 2 * p // PAIRS, :],
                                            bank[p % 2][:, 0:6 * D].rearrange("p (r q d) -> p q r d", r=2, q=3)[:, 0:2],
                                            bias2, ALU.add).then_inc(qk_kept, 1)
                    if lag and p == 0:
                        sums_rows(b, s - 1)
                    if lag and p == 1:
                        set_s(b, s - 1, kept)
                    if beside is not None:
                        add_x2(b - 1, beside, p)
                dve.wait_ge(ev_done, t + 2)
                for a in range(2):
                    nc.vector.tensor_reduce(mx[0][halves[a], :], own(e_ps, a), axis=AX.X, op=ALU.max).then_inc(v_max, 1)
                dve.wait_ge(v_exp, t + 1)
                for a in range(2):
                    dve.wait_ge(v_max, 2 * t + a + 2)
                    nc.vector.tensor_tensor(es[0][halves[a], :, :], own(e_ps, a), over(mx[0], D)[halves[a], :, :],
                                            ALU.subtract).then_inc(v_sub, 1)

            def round_of_steps(b, r):
                for u in range(ROUND):
                    s = r * ROUND + u
                    kept = (b - 1) * KEPT + s - BESIDE if u > BESIDE or later(r) else None
                    step(b, s, u > 0 or later(r), r * BESIDE + u - 1 if u > 0 else None, kept)

            def shifted(b, i, k):
                n = b * GROUPS + i * 2 + k
                dve.wait_ge(eh_done, n + 2)
                for a in range(2):
                    nc.vector.tensor_reduce(mx[k][halves[a], :], own(e_bank[k], a), axis=AX.X,
                                            op=ALU.max).then_inc(h_max, 1)
                for a in range(2):
                    dve.wait_ge(h_max, 2 * n + a + 2)
                    nc.vector.tensor_tensor(es[k][halves[a], :, :], own(e_bank[k], a), over(mx[k], D)[halves[a], :, :],
                                            ALU.subtract).then_inc(h_sub[k], 1)

            def sums_cols(b, i, k):
                n = b * GROUPS + i * 2 + k
                dve.wait_ge(h_exp, n + 2)
                nc.vector.tensor_reduce(sm[k][:], pr[k][:], axis=AX.X, op=ALU.add).then_inc(h_sum, 1)
                dve.wait_ge(h_sum, n + 2)
                nc.vector.reciprocal(rs[k][:], sm[k][:]).then_inc(h_rs, 1)

            def add_s(b, i, k):
                dve.wait_ge(oh_done[k], b * TURNS + i + 2)
                cols = S[:, :, bass.ds((i * 2 + k) * GW, GW)]
                nc.vector.tensor_tensor(cols, oh_bank[k][:].rearrange("p (w j) -> p j w", w=GW), cols,
                                        ALU.add).then_inc(s_added[k], 1)

            def channels(b, i, q):
                dve.wait_ge(ch_done, b * NCG + i * 4 + q + 2)
                nc.vector.tensor_copy(channels_of(i, q), ch_bank[q].rearrange("p (c w) -> p w c", c=CG))\
                  .then_inc(ch_kept_dve, 1)

            def turn(b, i, units, first=False):
                for k in range(2):
                    shifted(b, i + 1, k)
                    if k == 1:
                        add_s(b, i, 0)
                    elif not first:
                        add_s(b, i - 1, 1)
                    sums_cols(b, i + 1, k)
                    for s, o in units[k:k + 1]:
                        add_x2(b - 1, s, o)

            def middle(b, second):
                for q in (0, 2):
                    channels(b, 0, q)
                sums_rows(b, STEPS - 1)
                for q in (0, 2):
                    channels(b, 1, q)
                set_s(b, STEPS - 1, b * KEPT if second else None)
                for o, i0 in enumerate(EARLY_AT):
                    with dve.Fori(i0 - 1, i0 + 1) as i:
                        for q in (0, 2):
                            channels(b, i, q)
                    if second:
                        add_x2(b - 1, EARLY, o)
                dve.wait_ge(s_set, (b + 1) * STEPS + 1)
                for k in range(2):
                    shifted(b, 0, k)
                for k in range(2):
                    sums_cols(b, 0, k)
                if second:
                    add_x2(b - 1, EARLY, 3)
                    def late_step(n, first=False):
                        turn(b, 2 * n, [(EARLY + 1 + n, 0), (EARLY + 1 + n, 1)], first)
                        turn(b, 2 * n + 1, [(EARLY + 1 + n, 2), (EARLY + 1 + n, 3)])
                    late_step(0, True)
                    with dve.Fori(1, LATE - 1) as n:
                        late_step(n)
                else:
                    turn(b, 0, [], True)
                with dve.Fori(2 * (LATE - 1) if second else 1, TURNS - 1) as i:
                    turn(b, i, [])
                add_s(b, TURNS - 2, 1)
                for k in range(2):
                    add_s(b, TURNS - 1, k)

            def image(b, second):
                if second:
                    round_of_steps(b, 0)
                    with dve.Fori(1, STEPS // ROUND) as r:
                        round_of_steps(b, r)
                else:
                    step(b, 0, False, None)
                    with dve.Fori(1, STEPS) as s:
                        step(b, s, True, None)
                middle(b, second)

            opened(dve, qk_kept, v_max, v_sub, v_sum, v_rs, s_set, added, ch_kept_dve,
                   h_max, h_sum, h_rs, *h_sub, *s_added)
            nc.vector.memset(bd[:], 0.0).then_inc(consts_ready, 1)
            dve.wait_ge(weights_loaded, 16 * N_WEIGHTS)
            nc.vector.tensor_scalar(wo_raw, wo_raw, gam[:], None, ALU.mult).then_inc(consts_ready, 1)
            dve.wait_ge(consts_ready, 2)
            nc.vector.tensor_copy(wo_hi[:], wo_raw).then_inc(consts_ready, 1)
            dve.wait_ge(consts_ready, 3)
            nc.vector.tensor_tensor(wo_lo[:], wo_raw, wo_hi[:].bitcast(F32), ALU.subtract).then_inc(consts_ready, 1)
            dve.wait_ge(consts_ready, 4)
            image(0, False)
            with dve.Fori(1, B) as b:
                image(b, True)

            def finish(s, n, turn):
                for o in range(OC):
                    add_x(B - 1, s, o, x_end[n][o], end_loaded[n][o], loads(n, turn), proj_ps2 if o % 2 else proj_ps)

            with dve.Fori(0, STEPS // SETS) as r:
                for n in range(SETS):
                    finish(r * SETS + n, n, r + 1)
            for n in range(STEPS % SETS):
                finish(STEPS - STEPS % SETS + n, n, STEPS // SETS + 1)


def kernel(x, L0_conv_qkv_w, L0_conv_qkv_b, L0_conv_out_w, L0_conv_out_b, L0_conv_gamma):
    import numpy as np
    import concourse.bacc as bacc
    from concourse.bass_utils import run_bass_kernel_spmd

    arrays = {
        "x": np.ascontiguousarray(x),
        "wqkv_t": np.ascontiguousarray(np.asarray(L0_conv_qkv_w).T),
        "qkv_b": np.ascontiguousarray(L0_conv_qkv_b),
        "wo_t": np.ascontiguousarray(np.asarray(L0_conv_out_w).T),
        "out_b": np.ascontiguousarray(np.asarray(L0_conv_out_b).reshape(OC, P).T),
        "gamma": np.ascontiguousarray(L0_conv_gamma).reshape(1),
    }
    nc = bacc.Bacc("TRN2", target_bir_lowering=False, num_devices=1)
    aps = [nc.dram_tensor(n, a.shape, mybir.dt.from_np(a.dtype), kind="ExternalInput").ap() for n, a in arrays.items()]
    out = nc.dram_tensor("out", (B, C, H, W), F32, kind="ExternalOutput").ap()
    axial_attention(nc, *aps, out)
    r = run_bass_kernel_spmd(nc, [arrays], core_ids=[0])
    return r.results[0]["out"]
```
